# Optimizing a Trainium2 kernel written in Bass

```python
import numpy as np
import jax
import jax.numpy as jnp

def _softmax(x, axis=-1):
    return jax.nn.softmax(x, axis=axis)

def _gelu(x):
    return jax.nn.gelu(x, approximate=True)

def _silu(x):
    return jax.nn.silu(x)

def _sigmoid(x):
    return jax.nn.sigmoid(x)

def _layernorm(x, axis=-1, eps=1e-05):
    m = jnp.mean(x, axis=axis, keepdims=True)
    v = jnp.var(x, axis=axis, keepdims=True)
    return (x - m) / jnp.sqrt(v + eps)

def _scatter_add(tgt, idx, src, axis=0):
    return tgt.at[idx].add(src)

def _segment_sum(src, seg, n):
    return jax.ops.segment_sum(src, seg, n)
kernel_name = 'mk_rec_standalone_d1_rec_r8_397bb0'

def setup_inputs(seed: int=0):
    np.random.seed(seed)
    _w = jnp.asarray

    def _rec_inputs():
        import jax
        import jax.numpy as jnp
        _rk = jax.random.key(seed)
        r_items = jnp.stack([jax.random.randint(jax.random.fold_in(jax.random.fold_in(_rk, 1), 0), (2048,), 76, 99919, jnp.int32), jax.random.randint(jax.random.fold_in(jax.random.fold_in(_rk, 1), 1), (2048,), 55, 99454, jnp.int32), jax.random.randint(jax.random.fold_in(jax.random.fold_in(_rk, 1), 2), (2048,), 29, 99986, jnp.int32), jax.random.randint(jax.random.fold_in(jax.random.fold_in(_rk, 1), 3), (2048,), 67, 99935, jnp.int32), jax.random.randint(jax.random.fold_in(jax.random.fold_in(_rk, 1), 4), (2048,), 209, 99887, jnp.int32), jax.random.randint(jax.random.fold_in(jax.random.fold_in(_rk, 1), 5), (2048,), 176, 99942, jnp.int32), jax.random.randint(jax.random.fold_in(jax.random.fold_in(_rk, 1), 6), (2048,), 1, 99939, jnp.int32), jax.random.randint(jax.random.fold_in(jax.random.fold_in(_rk, 1), 7), (2048,), 31, 99945, jnp.int32), jax.random.randint(jax.random.fold_in(jax.random.fold_in(_rk, 1), 8), (2048,), 95, 99951, jnp.int32), jax.random.randint(jax.random.fold_in(jax.random.fold_in(_rk, 1), 9), (2048,), 13, 12482, jnp.int32), jax.random.randint(jax.random.fold_in(jax.random.fold_in(_rk, 1), 10), (2048,), 70, 99701, jnp.int32), jax.random.randint(jax.random.fold_in(jax.random.fold_in(_rk, 1), 11), (2048,), 146, 99964, jnp.int32), jax.random.randint(jax.random.fold_in(jax.random.fold_in(_rk, 1), 12), (2048,), 39, 12467, jnp.int32), jax.random.randint(jax.random.fold_in(jax.random.fold_in(_rk, 1), 13), (2048,), 6, 99887, jnp.int32), jax.random.randint(jax.random.fold_in(jax.random.fold_in(_rk, 1), 14), (2048,), 323, 99835, jnp.int32), jax.random.randint(jax.random.fold_in(jax.random.fold_in(_rk, 1), 15), (2048,), 131, 99917, jnp.int32), jax.random.randint(jax.random.fold_in(jax.random.fold_in(_rk, 1), 16), (2048,), 28, 99865, jnp.int32), jax.random.randint(jax.random.fold_in(jax.random.fold_in(_rk, 1), 17), (2048,), 20, 99962, jnp.int32), jax.random.randint(jax.random.fold_in(jax.random.fold_in(_rk, 1), 18), (2048,), 86, 99873, jnp.int32), jax.random.randint(jax.random.fold_in(jax.random.fold_in(_rk, 1), 19), (2048,), 18, 12488, jnp.int32), jax.random.randint(jax.random.fold_in(jax.random.fold_in(_rk, 1), 20), (2048,), 17, 99987, jnp.int32), jax.random.randint(jax.random.fold_in(jax.random.fold_in(_rk, 1), 21), (2048,), 231, 99946, jnp.int32), jax.random.randint(jax.random.fold_in(jax.random.fold_in(_rk, 1), 22), (2048,), 264, 99913, jnp.int32), jax.random.randint(jax.random.fold_in(jax.random.fold_in(_rk, 1), 23), (2048,), 32, 99861, jnp.int32), jax.random.randint(jax.random.fold_in(jax.random.fold_in(_rk, 1), 24), (2048,), 78, 99953, jnp.int32), jax.random.randint(jax.random.fold_in(jax.random.fold_in(_rk, 1), 25), (2048,), 90, 12459, jnp.int32), jax.random.randint(jax.random.fold_in(jax.random.fold_in(_rk, 1), 26), (2048,), 98, 99911, jnp.int32), jax.random.randint(jax.random.fold_in(jax.random.fold_in(_rk, 1), 27), (2048,), 104, 99805, jnp.int32), jax.random.randint(jax.random.fold_in(jax.random.fold_in(_rk, 1), 28), (2048,), 71, 99870, jnp.int32), jax.random.randint(jax.random.fold_in(jax.random.fold_in(_rk, 1), 29), (2048,), 185, 99594, jnp.int32), jax.random.randint(jax.random.fold_in(jax.random.fold_in(_rk, 1), 30), (2048,), 394, 99938, jnp.int32), jax.random.randint(jax.random.fold_in(jax.random.fold_in(_rk, 1), 31), (2048,), 116, 99794, jnp.int32), jax.random.randint(jax.random.fold_in(jax.random.fold_in(_rk, 1), 32), (2048,), 100, 99954, jnp.int32), jax.random.randint(jax.random.fold_in(jax.random.fold_in(_rk, 1), 33), (2048,), 17, 99946, jnp.int32), jax.random.randint(jax.random.fold_in(jax.random.fold_in(_rk, 1), 34), (2048,), 46, 99945, jnp.int32), jax.random.randint(jax.random.fold_in(jax.random.fold_in(_rk, 1), 35), (2048,), 19, 99949, jnp.int32), jax.random.randint(jax.random.fold_in(jax.random.fold_in(_rk, 1), 36), (2048,), 148, 99807, jnp.int32), jax.random.randint(jax.random.fold_in(jax.random.fold_in(_rk, 1), 37), (2048,), 64, 99906, jnp.int32), jax.random.randint(jax.random.fold_in(jax.random.fold_in(_rk, 1), 38), (2048,), 53, 99948, jnp.int32), jax.random.randint(jax.random.fold_in(jax.random.fold_in(_rk, 1), 39), (2048,), 14, 99978, jnp.int32), jax.random.randint(jax.random.fold_in(jax.random.fold_in(_rk, 1), 40), (2048,), 88, 99969, jnp.int32), jax.random.randint(jax.random.fold_in(jax.random.fold_in(_rk, 1), 41), (2048,), 1, 99884, jnp.int32), jax.random.randint(jax.random.fold_in(jax.random.fold_in(_rk, 1), 42), (2048,), 79, 99847, jnp.int32), jax.random.randint(jax.random.fold_in(jax.random.fold_in(_rk, 1), 43), (2048,), 45, 99942, jnp.int32), jax.random.randint(jax.random.fold_in(jax.random.fold_in(_rk, 1), 44), (2048,), 5, 12484, jnp.int32), jax.random.randint(jax.random.fold_in(jax.random.fold_in(_rk, 1), 45), (2048,), 213, 99855, jnp.int32), jax.random.randint(jax.random.fold_in(jax.random.fold_in(_rk, 1), 46), (2048,), 142, 99809, jnp.int32), jax.random.randint(jax.random.fold_in(jax.random.fold_in(_rk, 1), 47), (2048,), 62, 99821, jnp.int32), jax.random.randint(jax.random.fold_in(jax.random.fold_in(_rk, 1), 48), (2048,), 3, 99964, jnp.int32), jax.random.randint(jax.random.fold_in(jax.random.fold_in(_rk, 1), 49), (2048,), 82, 99919, jnp.int32)], axis=1)
        r_inputs = jnp.stack([jax.random.randint(jax.random.fold_in(jax.random.fold_in(_rk, 2), 0), (2048,), 55, 99965, jnp.int32), jax.random.randint(jax.random.fold_in(jax.random.fold_in(_rk, 2), 1), (2048,), 48, 12493, jnp.int32), jax.random.randint(jax.random.fold_in(jax.random.fold_in(_rk, 2), 2), (2048,), 149, 99818, jnp.int32), jax.random.randint(jax.random.fold_in(jax.random.fold_in(_rk, 2), 3), (2048,), 64, 99943, jnp.int32), jax.random.randint(jax.random.fold_in(jax.random.fold_in(_rk, 2), 4), (2048,), 83, 99948, jnp.int32), jax.random.randint(jax.random.fold_in(jax.random.fold_in(_rk, 2), 5), (2048,), 54, 99999, jnp.int32), jax.random.randint(jax.random.fold_in(jax.random.fold_in(_rk, 2), 6), (2048,), 215, 99939, jnp.int32), jax.random.randint(jax.random.fold_in(jax.random.fold_in(_rk, 2), 7), (2048,), 95, 99911, jnp.int32), jax.random.randint(jax.random.fold_in(jax.random.fold_in(_rk, 2), 8), (2048,), 33, 99809, jnp.int32), jax.random.randint(jax.random.fold_in(jax.random.fold_in(_rk, 2), 9), (2048,), 67, 99845, jnp.int32), jax.random.randint(jax.random.fold_in(jax.random.fold_in(_rk, 2), 10), (2048,), 35, 99948, jnp.int32), jax.random.randint(jax.random.fold_in(jax.random.fold_in(_rk, 2), 11), (2048,), 56, 99973, jnp.int32), jax.random.randint(jax.random.fold_in(jax.random.fold_in(_rk, 2), 12), (2048,), 30, 99941, jnp.int32), jax.random.randint(jax.random.fold_in(jax.random.fold_in(_rk, 2), 13), (2048,), 97, 99859, jnp.int32), jax.random.randint(jax.random.fold_in(jax.random.fold_in(_rk, 2), 14), (2048,), 23, 99998, jnp.int32), jax.random.randint(jax.random.fold_in(jax.random.fold_in(_rk, 2), 15), (2048,), 116, 99994, jnp.int32), jax.random.randint(jax.random.fold_in(jax.random.fold_in(_rk, 2), 16), (2048,), 148, 12495, jnp.int32), jax.random.randint(jax.random.fold_in(jax.random.fold_in(_rk, 2), 17), (2048,), 206, 99747, jnp.int32), jax.random.randint(jax.random.fold_in(jax.random.fold_in(_rk, 2), 18), (2048,), 37, 99628, jnp.int32), jax.random.randint(jax.random.fold_in(jax.random.fold_in(_rk, 2), 19), (2048,), 324, 12483, jnp.int32), jax.random.randint(jax.random.fold_in(jax.random.fold_in(_rk, 2), 20), (2048,), 89, 12495, jnp.int32), jax.random.randint(jax.random.fold_in(jax.random.fold_in(_rk, 2), 21), (2048,), 68, 99881, jnp.int32), jax.random.randint(jax.random.fold_in(jax.random.fold_in(_rk, 2), 22), (2048,), 2, 99711, jnp.int32), jax.random.randint(jax.random.fold_in(jax.random.fold_in(_rk, 2), 23), (2048,), 311, 99742, jnp.int32), jax.random.randint(jax.random.fold_in(jax.random.fold_in(_rk, 2), 24), (2048,), 53, 99950, jnp.int32), jax.random.randint(jax.random.fold_in(jax.random.fold_in(_rk, 2), 25), (2048,), 190, 99982, jnp.int32), jax.random.randint(jax.random.fold_in(jax.random.fold_in(_rk, 2), 26), (2048,), 216, 99910, jnp.int32), jax.random.randint(jax.random.fold_in(jax.random.fold_in(_rk, 2), 27), (2048,), 148, 99953, jnp.int32), jax.random.randint(jax.random.fold_in(jax.random.fold_in(_rk, 2), 28), (2048,), 137, 99935, jnp.int32), jax.random.randint(jax.random.fold_in(jax.random.fold_in(_rk, 2), 29), (2048,), 122, 12485, jnp.int32), jax.random.randint(jax.random.fold_in(jax.random.fold_in(_rk, 2), 30), (2048,), 8, 99927, jnp.int32), jax.random.randint(jax.random.fold_in(jax.random.fold_in(_rk, 2), 31), (2048,), 13, 99979, jnp.int32), jax.random.randint(jax.random.fold_in(jax.random.fold_in(_rk, 2), 32), (2048,), 120, 99930, jnp.int32), jax.random.randint(jax.random.fold_in(jax.random.fold_in(_rk, 2), 33), (2048,), 49, 99972, jnp.int32), jax.random.randint(jax.random.fold_in(jax.random.fold_in(_rk, 2), 34), (2048,), 134, 99879, jnp.int32), jax.random.randint(jax.random.fold_in(jax.random.fold_in(_rk, 2), 35), (2048,), 12, 99958, jnp.int32), jax.random.randint(jax.random.fold_in(jax.random.fold_in(_rk, 2), 36), (2048,), 168, 12497, jnp.int32), jax.random.randint(jax.random.fold_in(jax.random.fold_in(_rk, 2), 37), (2048,), 57, 99894, jnp.int32), jax.random.randint(jax.random.fold_in(jax.random.fold_in(_rk, 2), 38), (2048,), 231, 99987, jnp.int32), jax.random.randint(jax.random.fold_in(jax.random.fold_in(_rk, 2), 39), (2048,), 35, 99956, jnp.int32), jax.random.randint(jax.random.fold_in(jax.random.fold_in(_rk, 2), 40), (2048,), 23, 12490, jnp.int32), jax.random.randint(jax.random.fold_in(jax.random.fold_in(_rk, 2), 41), (2048,), 114, 99951, jnp.int32), jax.random.randint(jax.random.fold_in(jax.random.fold_in(_rk, 2), 42), (2048,), 0, 99894, jnp.int32), jax.random.randint(jax.random.fold_in(jax.random.fold_in(_rk, 2), 43), (2048,), 158, 99699, jnp.int32), jax.random.randint(jax.random.fold_in(jax.random.fold_in(_rk, 2), 44), (2048,), 28, 99839, jnp.int32), jax.random.randint(jax.random.fold_in(jax.random.fold_in(_rk, 2), 45), (2048,), 5, 99956, jnp.int32), jax.random.randint(jax.random.fold_in(jax.random.fold_in(_rk, 2), 46), (2048,), 69, 99986, jnp.int32), jax.random.randint(jax.random.fold_in(jax.random.fold_in(_rk, 2), 47), (2048,), 4, 99981, jnp.int32), jax.random.randint(jax.random.fold_in(jax.random.fold_in(_rk, 2), 48), (2048,), 55, 99931, jnp.int32), jax.random.randint(jax.random.fold_in(jax.random.fold_in(_rk, 2), 49), (2048,), 82, 99978, jnp.int32)], axis=1)
        r_alias_inputs = jax.random.randint(jax.random.fold_in(_rk, 3), (2048, 50), 0, 50, jnp.int32)
        return (r_items, r_inputs, r_alias_inputs)
    r_items, r_inputs, r_alias_inputs = _rec_inputs()

    def _L0_rec_setup():
        import jax, jax.numpy as jnp
        import numpy as np
        N = 12500
        D = 128
        B = 1024
        L = 50
        NNZ = 200000
        LAYERS = 2
        W_K = 12.0
        EPS = 1e-12

        def _l2norm(x):
            n = jnp.sqrt(jnp.sum(x * x, axis=-1, keepdims=True))
            return x / jnp.maximum(n, EPS)
        key = jax.random.key(seed)
        ks = jax.random.split(key, 12)
        stdv = 1.0 / np.sqrt(D)
        u = lambda k, shape: jax.random.uniform(k, shape, jnp.float32, -stdv, stdv)
        inp = {'items': jax.random.randint(ks[0], (B, L), 0, N), 'inputs': jax.random.randint(ks[1], (B, L), 0, N), 'alias_inputs': jax.random.randint(ks[2], (B, L), 0, L), 'adj_row': jnp.sort(jax.random.randint(ks[3], (NNZ,), 0, N)), 'adj_col': jax.random.randint(ks[4], (NNZ,), 0, N), 'adj_val': jax.random.uniform(ks[5], (NNZ,), jnp.float32), 'E': u(ks[6], (N, D)), 'pos_emb': u(ks[7], (L, D)), 'w1': u(ks[8], (2 * D, D)), 'w2': u(ks[9], (D, 1)), 'glu1_w': u(ks[10], (D, D)), 'glu1_b': jnp.zeros((D,), jnp.float32), 'glu2_w': u(ks[11], (D, D))}
        return inp
    _L0_rec_all = _L0_rec_setup()
    _L0_rec_in = {k: v for k, v in _L0_rec_all.items() if k in ('adj_row', 'adj_col', 'adj_val', 'E', 'pos_emb', 'w1', 'w2', 'glu1_w', 'glu1_b', 'glu2_w')}
    del _L0_rec_all
    return {'r_items': r_items, 'r_inputs': r_inputs, 'r_alias_inputs': r_alias_inputs, 'L0_rec_adj_row': _L0_rec_in['adj_row'], 'L0_rec_adj_col': _L0_rec_in['adj_col'], 'L0_rec_adj_val': _L0_rec_in['adj_val'], 'L0_rec_E': _L0_rec_in['E'], 'L0_rec_pos_emb': _L0_rec_in['pos_emb'], 'L0_rec_w1': _L0_rec_in['w1'], 'L0_rec_w2': _L0_rec_in['w2'], 'L0_rec_glu1_w': _L0_rec_in['glu1_w'], 'L0_rec_glu1_b': _L0_rec_in['glu1_b'], 'L0_rec_glu2_w': _L0_rec_in['glu2_w']}

def reference(r_items, r_inputs, r_alias_inputs, L0_rec_adj_row, L0_rec_adj_col, L0_rec_adj_val, L0_rec_E, L0_rec_pos_emb, L0_rec_w1, L0_rec_w2, L0_rec_glu1_w, L0_rec_glu1_b, L0_rec_glu2_w):
    import jax
    import jax.numpy as jnp

    def _L0_rec_ref(items, inputs, alias_inputs, adj_row, adj_col, adj_val, E, pos_emb, w1, w2, glu1_w, glu1_b, glu2_w):
        import jax, jax.numpy as jnp
        import numpy as np
        N = 12500
        D = 128
        B = 1024
        L = 50
        NNZ = 200000
        LAYERS = 2
        W_K = 12.0
        EPS = 1e-12

        def _l2norm(x):
            n = jnp.sqrt(jnp.sum(x * x, axis=-1, keepdims=True))
            return x / jnp.maximum(n, EPS)

        def spmm(h):
            return jax.ops.segment_sum(adj_val[:, None] * h[adj_col], adj_row, num_segments=N)
        h = E
        acc = E
        for _ in range(LAYERS):
            h = _l2norm(spmm(h))
            acc = acc + h
        graph_item_embs = acc / (LAYERS + 1)
        hidden = graph_item_embs[items]
        seq_hidden = jnp.take_along_axis(hidden, alias_inputs[..., None], axis=1)
        mask = (inputs != 0).astype(seq_hidden.dtype)[..., None]
        hs = jnp.sum(seq_hidden * mask, axis=1) / jnp.sum(mask, axis=1)
        pos = jnp.flip(pos_emb, axis=0)
        pos_b = jnp.broadcast_to(pos[None], (seq_hidden.shape[0], L, D))
        nh = jnp.tanh(jnp.concatenate([pos_b, seq_hidden], axis=-1) @ w1)
        nh = jax.nn.sigmoid(nh @ glu1_w.T + glu1_b + (hs @ glu2_w.T)[:, None, :])
        beta = nh @ w2 * mask
        sess_emb = jnp.sum(beta * seq_hidden, axis=1)
        select = W_K * _l2norm(sess_emb)
        scores = select @ _l2norm(graph_item_embs).T
        return scores
    y = _L0_rec_ref(r_items, r_inputs, r_alias_inputs, L0_rec_adj_row, L0_rec_adj_col, L0_rec_adj_val, L0_rec_E, L0_rec_pos_emb, L0_rec_w1, L0_rec_w2, L0_rec_glu1_w, L0_rec_glu1_b, L0_rec_glu2_w)
    return y

_drawn_inputs = setup_inputs


def setup_inputs(seed=0):
    import zlib

    import numpy as np

    out = dict(_drawn_inputs(seed))
    spreads = {'L0_rec_glu1_b': (0.0, 0.8)}
    factors = {'L0_rec_pos_emb': 8.0,
     'L0_rec_w1': 7.893,
     'L0_rec_w2': 5.146,
     'L0_rec_glu1_w': 6.606,
     'L0_rec_glu2_w': 26.914}
    for name, (base, spread) in spreads.items():
        noise = np.random.default_rng([zlib.crc32(name.encode()), seed]).standard_normal(out[name].shape)
        drawn = base * np.exp(spread * noise) if base else spread * noise
        out[name] = jnp.asarray(drawn.astype(out[name].dtype))
    for name, factor in factors.items():
        out[name] = (out[name] * factor).astype(out[name].dtype)
    return out
```

```python
from contextlib import ExitStack

import concourse.bass as bass
from concourse import mybir

F32 = mybir.dt.float32
I32 = mybir.dt.int32
U32 = mybir.dt.uint32
ALU = mybir.AluOpType
ACT = mybir.ActivationFunctionType
AX_X = mybir.AxisListType.X

P = 128
EPS = 1e-12
W_K = 12.0
LAYERS = 2
FAR = 1e10


def build(nc, items, inputs, alias, adj_row, adj_col, adj_val, E, pos_emb, w1, w2,
          glu1_w, glu1_b, glu2_w, out):
    N, D = E.shape
    S, L = items.shape
    NNZ = adj_row.shape[0]
    assert D == P and S % P == 0 and L <= P

    TG = 8
    EG = TG * P
    NG = -(-NNZ // EG)
    HG = NG // 2
    TAIL = NNZ - (NG - 1) * EG
    TAIL_T = -(-TAIL // P)
    PAIRS = NG // 2 - 1
    assert NG == 2 * HG and HG <= P

    NT = -(-N // P)
    NQ = -(-NT // 4)
    NP_ = NT * P
    LAST_T = N - (NT - 1) * P
    assert NT == PAIRS + 1 and NT <= L * 2

    def quad(q):
        return min(4, NT - 4 * q)

    T = S // P
    CH = [list(range(4 * c, min(4 * c + 4, L))) for c in range(-(-L // 4))]
    NC = len(CH)
    assert T % 2 == 0 and NC % 2 == 1
    IDX_L = 10
    IDX_C = L // IDX_L

    SC = 500
    NS = N // SC
    BC = 3
    NB = -(-NS // BC)
    assert NS * SC == N and NS % 2 == 1 and NB % 2 == 1
    NS_A, NS_D = (NS + 1) // 2, NS // 2

    h1_dram = nc.dram_tensor("h1_rows", (NP_, D), F32).ap()
    graph_dram = nc.dram_tensor("graph_rows", (NP_, 2 * D), F32).ap()

    with ExitStack() as ctx:
        def sb(name, shape, dt=F32):
            return ctx.enter_context(nc.sbuf_tensor(name, shape, dt))

        def sem(name):
            return ctx.enter_context(nc.semaphore(name))

        sumT = sb("sumT", [P, N + P])
        seq0 = sb("seq0", [P, L * 2 * D])
        seq1 = sb("seq1", [P, L * 2 * D])
        seq = [x[:, :].rearrange("p (l d) -> p l d", l=L) for x in (seq0, seq1)]
        h1_rows = seq0[:, 0:NT * D].rearrange("p (t d) -> p t d", d=D)
        base_rows = seq1[:, 0:NT * D].rearrange("p (t d) -> p t d", d=D)

        def raw(n, dt=F32):
            v = seq0[0:HG, 2 * EG * n:2 * EG * (n + 1)]
            return (v if dt is F32 else v.bitcast(dt)).rearrange("g (h n) -> g h n", h=2)

        row_i, col_i, val_f = raw(0, I32), raw(1, I32), raw(2)
        row_f, tmp_f, col_f = raw(3), raw(4), raw(5)

        work = sb("work", [P, 3 * TG * NG + 2 * TG * D])
        table = work[:, 0:3 * TG * NG].rearrange("p (q g) -> p q g", g=NG)
        gath = work[:, 3 * TG * NG:].rearrange("p (s j d) -> p s j d", s=2, j=TG)
        nh = work[:, 0:NC * 4 * P].rearrange("p (c n) -> p c n", c=NC)

        onehot_b = sb("onehot", [P, TG * P])
        onehot = onehot_b[:, :].rearrange("p (j r) -> p j r", j=TG)
        two = onehot_b[:, :].rearrange("p (s n) -> p s n", s=2)

        stage_b = sb("stage", [P, 2 * BC * SC])
        stage = stage_b[:, :].rearrange("p (s n) -> p s n", s=2)
        items_i = stage_b[:, 0:T * L].bitcast(I32)
        alias_i = stage_b[:, T * L:2 * T * L].bitcast(I32)
        inputs_i = stage_b[:, 2 * T * L:3 * T * L].bitcast(I32)
        pick = stage_b[:, 3 * T * L:3 * T * L + IDX_L * L].rearrange("p (l m) -> p l m", l=IDX_L)
        g1_out = stage_b[:, 0:8 * D].rearrange("p (s j d) -> p s j d", s=2, j=4)
        root = stage_b[:, 8 * D:16 * D].rearrange("p (s n) -> p s n", s=2)

        item_idx = sb("item_idx", [P, (T + 1) * L], U32)
        mask = sb("mask", [P, T * L])
        ident = sb("ident", [P, P])
        glu1T = sb("glu1T", [P, D])
        glu2T = sb("glu2T", [P, D])
        posT = sb("posT", [P, L])
        w2c = sb("w2c", [P, 1])
        b1c = sb("b1c", [P, 1])
        hs_acc = sb("hs_acc", [P, 4, D])
        sess_acc = sb("sess_acc", [P, 4, D])
        hsT = sb("hsT", [P, P])
        qT = sb("qT", [P, P])
        selT = sb("selT", [P, 2, P])
        rcnt3 = sb("rcnt3", [P, T])
        bm = sb("bm", [P, 2, 4])
        small = sb("small", [P, 8])
        norms = sb("norms", [P, 2, 4])
        rinv = sb("rinv", [P, 2, 4])
        idx_l = sb("idx_l", [P, 2, IDX_L])
        idx_slot = sb("idx_slot", [P, 2, TG], U32)
        edge_slot = sb("edge_slot", [P, 2, 2 * TG])
        sess_idx = sb("sess_idx", [P, 2, L], U32)
        sched_f = sb("sched_f", [HG, 2, 2])
        sched_i = sb("sched_i", [HG, 2], I32)
        iota = qT
        w1b = selT[:, 0, :]
        ones = selT[:, 1, :]
        sched = hs_acc[0:1, :, :].rearrange("o a b -> o (a b)")[:, 0:2 * NG].bitcast(I32)
        pos_sb, glu1_sb, glu2_sb, w1a = (sess_acc[:, i, :] for i in range(4))
        hs_row = hsT

        bank = [ctx.enter_context(nc.psum_tensor(f"bank{b}", [P, 512], F32)) for b in range(8)]

        s_pad = sem("s_pad")
        s_row, s_col, s_val = sem("s_row"), sem("s_col"), sem("s_val")
        s_w = sem("s_w")
        s_sess_in = sem("s_sess_in")
        s_base = sem("s_base")
        s_const = sem("s_const")
        s_ones = sem("s_ones")
        s_colf = sem("s_colf")
        s_rel = sem("s_rel")
        s_tab_t = sem("s_tab_t")
        s_tab = sem("s_tab")
        s_sched_t, s_sched = sem("s_sched_t"), sem("s_sched")
        s_w_t, s_w_c = sem("s_w_t"), sem("s_w_c")
        s_mask = sem("s_mask")
        s_staged = sem("s_staged")
        s_gath = [sem("s_gath0"), sem("s_gath1")]
        s_onehot = sem("s_onehot")
        s_window = sem("s_window")
        s_group = sem("s_group")
        s_sq = sem("s_sq")
        s_fin = sem("s_fin")
        s_norm = sem("s_norm")
        s_rows = sem("s_rows")
        s_h1 = sem("s_h1")
        s_zero = sem("s_zero")
        s_gt, s_gtc = sem("s_gt"), sem("s_gtc")
        s_g1, s_g1c = sem("s_g1"), sem("s_g1c")
        s_gst = [sem("s_gst0"), sem("s_gst1")]
        s_gr = sem("s_gr")
        s_nsq, s_nsum = sem("s_nsq"), sem("s_nsum")
        s_nroot, s_gn = sem("s_nroot"), sem("s_gn")
        s_sidx_pad = sem("s_sidx_pad")
        s_sidx = sem("s_sidx")
        s_land = [[sem(f"s_land{i}_{c}") for c in range(NC)] for i in range(2)]
        s_g1t = sem("s_g1t")
        s_tanh = sem("s_tanh")
        s_mm2, s_qadd, s_sig = sem("s_mm2"), sem("s_qadd"), sem("s_sig")
        s_beta = sem("s_beta")
        s_free = sem("s_free")
        s_link, s_dec, s_pick = sem("s_link"), sem("s_dec"), sem("s_pick")
        s_nclip, s_bm, s_hsum, s_hred, s_sred = (sem(x) for x in ("s_nclip", "s_bm", "s_hsum", "s_hred", "s_sred"))
        s_hs, s_hst, s_hsT, s_q, s_qT = (sem(x) for x in ("s_hs", "s_hst", "s_hsT", "s_q", "s_qT"))
        s_n2, s_nn, s_sel, s_selt, s_selT = (sem(x) for x in ("s_n2", "s_nn", "s_sel", "s_selt", "s_selT"))
        s_score = sem("s_score")
        s_evA, s_evD = sem("s_evA"), sem("s_evD")
        s_pool, s_sp = sem("s_pool"), sem("s_sp")
        s_out = [sem("s_out0"), sem("s_out1")]

        def edges(x, half):
            if half == 0:
                return x[0:HG * EG].rearrange("(g n) -> g n", n=EG)
            return x[HG * EG:(NG - 1) * EG].rearrange("(g n) -> g n", n=EG)

        def by_tile(x):
            return x.rearrange("(p t) l -> p (t l)", t=T)

        graph_v = graph_dram.rearrange("(t p) c -> p t c", p=P)
        h1_v = h1_dram.rearrange("(t p) c -> p t c", p=P)
        out_v = out.rearrange("(p t) n -> p t n", t=T)

        SLOT0 = HG * TG * 16
        SLOT1 = (HG - 1) * TG * 16 + TAIL_T * 16

        def groups(eng, body, pair_extra=None):
            with eng.Fori(0, PAIRS) as i:
                body(i * 2, i, 0, TG)
                body(i * 2 + 1, i, 1, TG)
                if pair_extra is not None:
                    pair_extra(i)
            body(NG - 2, PAIRS, 0, TG)
            body(NG - 1, PAIRS, 1, TAIL_T)
            if pair_extra is not None:
                pair_extra(PAIRS)

        def session_steps(eng, step):
            step(0, 0, 0, True, False, False)
            step(1, 1, 0, True, True, False)
            step(2, 0, 1, True, True, True)
            step(3, 1, 1, True, True, True)
            with eng.Fori(2, T // 2) as v:
                step(v * 2, 0, v, True, True, True)
                step(v * 2 + 1, 1, v, True, True, True)
            step(T, 0, T // 2, False, True, True)
            step(T + 1, 1, T // 2, False, False, True)

        block = ctx.enter_context(nc.Block())

        @block.sync
        def _(sp):
            for x, dst, s in ((adj_col, col_i, s_col), (adj_row, row_i, s_row), (adj_val, val_f, s_val)):
                sp.dma_start(dst[:, 0, :], edges(x, 0)).then_inc(s, 16)
                if x is adj_col:
                    sp.wait_ge(s_pad, 3)
                sp.dma_start(dst[0:HG - 1, 1, :], edges(x, 1)).then_inc(s, 16)
                sp.dma_start(dst[HG - 1:HG, 1, 0:TAIL],
                             x[(NG - 1) * EG:NNZ].rearrange("(g n) -> g n", g=1)).then_inc(s, 16)
            for dst, src in ((w1a, w1[0:D, :]), (w1b, w1[D:2 * D, :]), (pos_sb[0:L, :], pos_emb),
                             (glu1_sb, glu1_w), (glu2_sb, glu2_w), (w2c[:, :], w2),
                             (b1c[:, :], glu1_b.rearrange("(p o) -> p o", o=1))):
                sp.dma_start(dst, src).then_inc(s_w, 16)
            for dst, src in ((items_i, items), (alias_i, alias), (inputs_i, inputs)):
                sp.dma_start(dst, by_tile(src)).then_inc(s_sess_in, 16)
            sp.wait_ge(s_pad, 4)
            sp.dma_start(base_rows[:, 0:NT - 1, :],
                         E[0:(NT - 1) * P, :].rearrange("(t p) d -> p t d", p=P)).then_inc(s_base, 16)
            sp.dma_start(base_rows[0:LAST_T, NT - 1, :], E[(NT - 1) * P:N, :]).then_inc(s_base, 16)

            for q in range(NQ):
                sp.wait_ge(s_rows, q + 1)
                sp.dma_start(h1_v[:, 4 * q:4 * q + quad(q), :],
                             h1_rows[:, 4 * q:4 * q + quad(q), :]).then_inc(s_h1, 16)
            for q in range(NQ):
                t0, t1 = 4 * q, 4 * q + quad(q)
                sp.wait_ge(s_rows, NQ + q + 1)
                sp.dma_start(graph_v[:, t0:t1, 0:D], base_rows[:, t0:t1, :]).then_inc(s_gr, 16)
                sp.wait_ge(s_g1c, q + 1)
                sp.dma_start(graph_v[:, t0:t1, D:2 * D],
                             g1_out[:, q % 2, 0:quad(q), :]).then_inc(s_gst[q % 2], 16)

            def step(s, par, half, A, B, C):
                if not C:
                    return
                u = s - 2
                for j in range(NB):
                    end = min(BC * (j + 1), NS)
                    sp.wait_ge(s_evA, u * NS_A + (end + 1) // 2)
                    sp.sem_inc(s_sp, 1)
                    sp.wait_ge(s_evD, u * NS_D + end // 2)
                    sp.sem_inc(s_sp, 1)
                    slot = (par + j) % 2
                    sp.dma_start(out_v[:, bass.ds(u, 1), BC * SC * j:SC * end],
                                 stage[:, slot:slot + 1, 0:SC * end - BC * SC * j]).then_inc(s_out[slot], 16)

            session_steps(sp, step)
            sp.wait_ge(s_out[0], 16 * (T * NB // 2))
            sp.wait_ge(s_out[1], 16 * (T * NB // 2))

        @block.gpsimd
        def _(pool):
            nc.gpsimd.iota(iota[:, :], [[1, P]], base=0, channel_multiplier=0,
                           allow_small_or_imprecise_dtypes=True).then_inc(s_const, 1)
            nc.gpsimd.iota(ident[:, :], [[1, P]], base=0, channel_multiplier=-1,
                           allow_small_or_imprecise_dtypes=True).then_inc(s_const, 1)
            pool.wait_ge(s_const, 2)
            nc.gpsimd.tensor_scalar(ident[:, :], ident[:, :], 0.0, None, ALU.is_equal).then_inc(s_const, 1)
            pool.wait_ge(s_col, 48)
            pool.wait_ge(s_const, 3)
            nc.gpsimd.tensor_copy(col_f, col_i).then_inc(s_colf, 1)
            pool.wait_ge(s_colf, 1)
            nc.gpsimd.tensor_scalar(raw(1), col_f, 0.0, float(N), ALU.is_lt, ALU.mult).then_inc(s_colf, 1)
            pool.wait_ge(s_colf, 2)
            nc.gpsimd.tensor_tensor(col_f, col_f, raw(1), ALU.add).then_inc(s_colf, 1)
            pool.wait_ge(s_colf, 3)
            nc.gpsimd.tensor_scalar(col_f, col_f, 0.0, float(N - 1), ALU.max, ALU.min).then_inc(s_colf, 1)
            pool.wait_ge(s_colf, 4)
            nc.gpsimd.memset(item_idx[:, T * L:(T + 1) * L], 0).then_inc(s_sidx_pad, 1)
            nc.gpsimd.memset(sumT[:, :], 0.0).then_inc(s_zero, 1)

            for layer in range(LAYERS):
                src = E if layer == 0 else h1_dram
                if layer == 1:
                    for q in range(NQ):
                        pool.wait_ge(s_fin, q + 1)
                        end = 512 * (q + 1) if q < NQ - 1 else N + P
                        nc.gpsimd.memset(sumT[:, 512 * q:end], 0.0).then_inc(s_zero, 1)
                    pool.wait_ge(s_h1, 16 * NQ)

                def gather(g, i, slot, tiles):
                    pool.wait_ge(s_staged, g + (layer * NG + 1))
                    pool.sem_inc(s_pool, 1)
                    for j in range(tiles):
                        nc.gpsimd.indirect_dma_start(
                            out=gath[:, slot, j, :], out_offset=None, in_=src,
                            in_offset=bass.IndirectOffsetOnAxis(ap=idx_slot[:, slot, j:j + 1], axis=0),
                        ).then_inc(s_gath[slot], 16)

                groups(pool, gather)

            pool.wait_ge(s_gr, 16 * NQ)
            pool.wait_ge(s_gst[0], 16 * ((NQ + 1) // 2))
            pool.wait_ge(s_gst[1], 16 * (NQ // 2))

            def step(s, par, half, A, B, C):
                if not A:
                    return
                pool.wait_ge(s_sidx, s + 1)
                pool.sem_inc(s_pool, 1)
                for c in range(NC):
                    if C:
                        pool.wait_ge(s_free, s * NC + (c + 1 - 2 * NC))
                        pool.sem_inc(s_pool, 1)
                    for l in CH[c]:
                        nc.gpsimd.indirect_dma_start(
                            out=seq[par][:, l, :], out_offset=None, in_=graph_dram,
                            in_offset=bass.IndirectOffsetOnAxis(ap=sess_idx[:, par, l:l + 1], axis=0),
                        ).then_inc(s_land[par][c], 16)

            session_steps(pool, step)

        @block.scalar
        def _(act):
            for n in range(12):
                q, h, jj = n // 4, n // 2 % 2, n % 2
                act.wait_ge(s_tab_t, n + 1)
                nc.scalar.copy(table[:, q * TG + 4 * jj:q * TG + 4 * jj + 4, h * HG:(h + 1) * HG],
                               bank[n % 4][:, 0:4 * HG].rearrange("p (j g) -> p j g", j=4)).then_inc(s_tab, 1)
            act.wait_ge(s_sched_t, 1)
            nc.scalar.copy(sched.rearrange("o (h g k) -> o h k g", h=2, k=2),
                           bank[4][0:1, 0:4 * HG].rearrange("o (h k g) -> o h k g", h=2, k=2)).then_inc(s_sched, 1)
            act.wait_ge(s_w_t, 1)
            nc.scalar.copy(hsT[:, 0:L], bank[5][:, 0:L]).then_inc(s_w_c, 1)
            nc.scalar.copy(glu1T[:, :], bank[6][:, 0:D]).then_inc(s_w_c, 1)
            nc.scalar.copy(glu2T[:, :], bank[6][:, D:2 * D]).then_inc(s_w_c, 1)
            act.wait_ge(s_w_t, 2)
            nc.scalar.copy(posT[:, :], bank[7][:, 0:L]).then_inc(s_w_c, 1)

            for layer in range(LAYERS):
                def stage_group(g, i, slot, tiles):
                    act.wait_ge(s_group, g + (layer * NG + 1))
                    nc.scalar.copy(idx_slot[:, slot, :], table[:, 0:TG, bass.ds(g, 1)]
                                   .rearrange("p q o -> p (q o)"))
                    nc.scalar.copy(edge_slot[:, slot, :], table[:, TG:3 * TG, bass.ds(g, 1)]
                                   .rearrange("p q o -> p (q o)")).then_inc(s_staged, 1)

                groups(act, stage_group)

                act.wait_ge(s_group, (layer + 1) * NG + 2)

                def square(q):
                    if q >= NQ:
                        return
                    if q >= 2:
                        act.wait_ge(s_fin, layer * NQ + q - 1)
                    w = quad(q) * P
                    nc.scalar.activation(two[:, q % 2, 0:w], sumT[:, 512 * q:512 * q + w],
                                         ACT.Square).then_inc(s_sq, 1)

                square(0)
                square(1)
                for q in range(NQ + 1):
                    if q < NQ:
                        act.wait_ge(s_fin, layer * NQ + q + 1)
                        if q >= 2:
                            act.wait_ge(s_rows, layer * NQ + q - 1)
                        nc.scalar.activation(norms[:, q % 2, 0:quad(q)], bank[2 + q % 2][:, 0:quad(q)],
                                             ACT.Sqrt).then_inc(s_norm, 1)
                        square(q + 2)
                    if layer == 1 and q >= 1:
                        r = q - 1
                        w = quad(r) * P
                        act.wait_ge(s_gt, r + 1)
                        nc.scalar.copy(sumT[:, 512 * r:512 * r + w], bank[4 + r % 2][:, 0:w]).then_inc(s_gtc, 1)

            act.wait_ge(s_sidx_pad, 1)
            nc.scalar.copy(sess_idx[:, 0, :], item_idx[:, 0:L]).then_inc(s_sidx, 1)

            def norm_square(q, par, w, first):
                if not first:
                    act.wait_ge(s_nsum, q - 1)
                nc.scalar.activation(two[:, par, 0:w], sumT[:, bass.ds(q * 512, w)], ACT.Square).then_inc(s_nsq, 1)

            def norm_root(q, par, w, first):
                act.wait_ge(s_nsum, q + 1)
                if not first:
                    act.wait_ge(s_gn, q - 1)
                nc.scalar.activation(root[:, par, 0:w], bank[par][:, 0:w], ACT.Sqrt).then_inc(s_nroot, 1)

            norm_square(0, 0, 512, True)
            norm_square(1, 1, 512, True)
            norm_root(0, 0, 512, True)
            norm_square(2, 0, 512, False)
            norm_root(1, 1, 512, True)
            norm_square(3, 1, 512, False)
            with act.Fori(1, NQ // 2 - 1) as v:
                norm_root(v * 2, 0, 512, False)
                norm_square(v * 2 + 2, 0, 512, False)
                norm_root(v * 2 + 1, 1, 512, False)
                norm_square(v * 2 + 3, 1, 512, False)
            norm_root(NQ - 3, 0, 512, False)
            norm_square(NQ - 1, 0, quad(NQ - 1) * P, False)
            norm_root(NQ - 2, 1, 512, False)
            norm_root(NQ - 1, 0, quad(NQ - 1) * P, False)

            def step(s, par, half, A, B, C):
                u, uh = s - 2, half - 1
                m0 = s * NC - NC
                if A:
                    nc.scalar.copy(sess_idx[:, 1 - par, :],
                                   item_idx[:, bass.ds(s * L + L, L)]).then_inc(s_sidx, 1)
                for c in range(NC):
                    if C:
                        k = 2 * c
                        j = k // BC
                        if k - 2 < BC * j:
                            n2 = (NB * par + j) // 2
                            if not (isinstance(s, int) and uh * NB + n2 == 0):
                                act.wait_ge(s_out[(par + j) % 2], uh * (16 * NB) + 16 * n2)
                        act.wait_ge(s_score, u * NS + (k + 1))
                        nc.scalar.copy(stage[:, (par + j) % 2, (k - BC * j) * SC:(k - BC * j + 1) * SC],
                                       bank[5][:, 0:SC]).then_inc(s_evA, 1)
                    if A:
                        act.wait_ge(s_g1t, s * NC + (c + 1))
                        if B:
                            act.wait_ge(s_mm2, m0 + (c + 1))
                        for i, l in enumerate(CH[c]):
                            last = nc.scalar.activation(nh[:, c, i * P:(i + 1) * P],
                                                        bank[(par + c) % 2][:, i * P:(i + 1) * P], ACT.Tanh,
                                                        bias=posT[:, L - 1 - l:L - l])
                        last.then_inc(s_tanh, 1)
                    if B:
                        w = len(CH[c]) * P
                        b = (par + 1 + c) % 2
                        act.wait_ge(s_qadd, m0 + (c + 1))
                        nc.scalar.activation(two[:, b, 0:w], two[:, b, 0:w], ACT.Sigmoid).then_inc(s_sig, 1)
                if A:
                    act.wait_ge(s_hst, s + 1)
                    nc.scalar.copy(hsT[:, :], bank[7][:, 0:P]).then_inc(s_hsT, 1)
                    act.wait_ge(s_q, s + 1)
                    nc.scalar.activation(qT[:, :], bank[7][:, P:2 * P], ACT.Identity,
                                         bias=b1c[:, 0:1]).then_inc(s_qT, 1)
                if B:
                    act.wait_ge(s_n2, s)
                    nc.scalar.activation(small[:, 1:2], small[:, 0:1], ACT.Sqrt).then_inc(s_nn, 1)
                    act.wait_ge(s_selt, s)
                    nc.scalar.copy(selT[:, (par + 1) % 2, :], bank[7][:, 2 * P:3 * P]).then_inc(s_selT, 1)

            session_steps(act, step)

        @block.vector
        def _(dve):
            last = slice((HG - 1) // 32 * 32, HG)
            nc.vector.memset(row_i[last, 1, :], N).then_inc(s_pad, 1)
            nc.vector.memset(col_i[last, 1, :], 0).then_inc(s_pad, 1)
            nc.vector.memset(val_f[last, 1, :], 0.0).then_inc(s_pad, 1)
            nc.vector.memset(base_rows[:, NT - 1, :], 0.0).then_inc(s_pad, 1)
            nc.vector.memset(ones, 1.0).then_inc(s_ones, 1)
            chain = [0]

            def link(ins):
                chain[0] += 1
                ins.then_inc(s_link, 1)
                dve.wait_ge(s_link, chain[0])

            nc.vector.memset(small[:, 7:8], 0.0).then_inc(s_group, 2)
            nc.vector.memset(small[:, 6:7], 0.0).then_inc(s_dec, 1)
            dve.wait_ge(s_row, 48)
            link(nc.vector.tensor_scalar(tmp_f, row_i, 0.0, None, ALU.is_lt))
            link(nc.vector.scalar_tensor_tensor(out=tmp_f, in0=row_i, scalar=float(N), in1=tmp_f,
                                                op0=ALU.is_ge, op1=ALU.add))
            link(nc.vector.scalar_tensor_tensor(out=row_f, in0=tmp_f, scalar=FAR, in1=row_i,
                                                op0=ALU.mult, op1=ALU.add))
            first, span = sched_f[:, :, 1], sched_f[:, :, 0]
            link(nc.vector.tensor_reduce(first, row_f, AX_X, ALU.min))
            link(nc.vector.tensor_scalar(first, first, float(N), None, ALU.min))
            for h in range(2):
                nc.vector.tensor_scalar(row_f[:, h, :], row_f[:, h, :], sched_f[:, h, 1:2], None,
                                        ALU.subtract).then_inc(s_rel, 1)
            dve.wait_ge(s_rel, 2)
            link(nc.vector.scalar_tensor_tensor(out=tmp_f, in0=tmp_f, scalar=-2 * FAR, in1=row_f,
                                                op0=ALU.mult, op1=ALU.add))
            link(nc.vector.tensor_reduce(span, tmp_f, AX_X, ALU.max))
            link(nc.vector.tensor_scalar(sched_i[:, :], span, 0.0, None, ALU.max))
            link(nc.vector.tensor_scalar(sched_i[:, :], sched_i[:, :], P.bit_length() - 1, None,
                                         ALU.arith_shift_right))
            nc.vector.tensor_scalar(span, sched_i[:, :], 1.0, None, ALU.add).then_inc(s_rel, 1)
            dve.wait_ge(s_sess_in, 48)
            link(nc.vector.tensor_scalar(mask[:, :], inputs_i, 0.0, None, ALU.not_equal))
            link(nc.vector.tensor_reduce(rcnt3[:, :], mask[:, :].rearrange("p (t l) -> p t l", t=T), AX_X,
                                         ALU.add))
            link(nc.vector.tensor_scalar(rcnt3[:, :], rcnt3[:, :], 3.0, None, ALU.mult))
            nc.vector.reciprocal(rcnt3[:, :], rcnt3[:, :]).then_inc(s_mask, 1)

            dve.wait_ge(s_sched, 1)
            dve.wait_ge(s_const, 3)
            dve.wait_ge(s_zero, 1)
            rounds = dve.alloc_register("dve_rounds")
            window = dve.alloc_register("dve_window")
            n_rounds = dve.alloc_register("dve_n_rounds")
            dve.reg_mov(rounds, 0)

            def layer_group(layer):
                def add_group(g, i, slot, tiles):
                    dve.wait_ge(s_staged, g + (layer * NG + 1))
                    dve.reg_load(n_rounds, sched[0:1, bass.ds(g * 2, 1)])
                    dve.reg_load(window, sched[0:1, bass.ds(g * 2 + 1, 1)])
                    with dve.Fori(0, n_rounds):
                        dve.reg_add(rounds, rounds, 1)
                        dve.wait_ge(s_dec, rounds)
                        for j in range(tiles):
                            last = nc.vector.tensor_scalar(onehot[:, j, :], iota[:, :], edge_slot[:, slot, j:j + 1],
                                                           edge_slot[:, slot, TG + j:TG + j + 1],
                                                           ALU.is_equal, ALU.mult)
                        last.then_inc(s_onehot, 1)
                        at = dve.snap(window, min_val=0, max_val=N)
                        dve.wait_ge(s_window, rounds)
                        nc.vector.tensor_tensor(sumT[:, bass.ds(at, P)], sumT[:, bass.ds(at, P)],
                                                bank[0][:, 0:P], ALU.add)
                        nc.vector.tensor_scalar(edge_slot[:, slot, 0:TG], edge_slot[:, slot, 0:TG],
                                                float(P), None, ALU.subtract).then_inc(s_dec, 1)
                        dve.reg_add(window, window, P)
                        dve.reg_alu(window, window, N, ALU.min)
                    nc.vector.memset(small[:, 7:8], 0.0).then_inc(s_group, 1)
                return add_group

            def item_indices(n, at, t_at):
                lane, neg = idx_l[:, 0, :], idx_l[:, 1, :]
                nc.vector.tensor_tensor(
                    pick, alias_i[:, bass.ds(at, IDX_L)].unsqueeze(2).broadcast_to([P, IDX_L, L]),
                    iota[:, 0:L].unsqueeze(1).broadcast_to([P, IDX_L, L]), ALU.is_equal).then_inc(s_pick, 1)
                dve.wait_ge(s_pick, n * 5 + 1)
                nc.vector.tensor_tensor(
                    pick, pick, items_i[:, bass.ds(t_at, L)].unsqueeze(1).broadcast_to([P, IDX_L, L]),
                    ALU.mult).then_inc(s_pick, 1)
                dve.wait_ge(s_pick, n * 5 + 2)
                nc.vector.tensor_reduce(lane, pick, AX_X, ALU.add).then_inc(s_pick, 1)
                dve.wait_ge(s_pick, n * 5 + 3)
                nc.vector.tensor_scalar(neg, lane, 0.0, float(N), ALU.is_lt, ALU.mult).then_inc(s_pick, 1)
                dve.wait_ge(s_pick, n * 5 + 4)
                nc.vector.tensor_tensor(lane, lane, neg, ALU.add).then_inc(s_pick, 1)
                dve.wait_ge(s_pick, n * 5 + 5)
                nc.vector.tensor_scalar(item_idx[:, bass.ds(at, IDX_L)], lane, 0.0, float(N - 1),
                                        ALU.max, ALU.min)

            add = layer_group(0)
            with dve.Fori(0, T) as t:
                with dve.Fori(0, IDX_C) as c:
                    i = t * IDX_C + c
                    add(i * 2, i, 0, TG)
                    item_indices(i, t * L + c * IDX_L, t * L)
                    add(i * 2 + 1, i, 1, TG)
            with dve.Fori(T * IDX_C, PAIRS) as i:
                add(i * 2, i, 0, TG)
                add(i * 2 + 1, i, 1, TG)
            add(NG - 2, PAIRS, 0, TG)
            add(NG - 1, PAIRS, 1, TAIL_T)

            def inverse(layer, q):
                dve.wait_ge(s_norm, layer * NQ + q + 1)
                w = quad(q)
                link(nc.vector.tensor_scalar(rinv[:, q % 2, 0:w], norms[:, q % 2, 0:w], EPS, None, ALU.max))
                link(nc.vector.reciprocal(rinv[:, q % 2, 0:w], rinv[:, q % 2, 0:w]))

            for q in range(NQ):
                inverse(0, q)
                w = quad(q)
                nc.vector.tensor_tensor(h1_rows[:, 4 * q:4 * q + w, :],
                                        bank[q % 2][:, 0:w * P].rearrange("p (j d) -> p j d", j=w),
                                        rinv[:, q % 2, 0:w].unsqueeze(2).broadcast_to([P, w, D]),
                                        ALU.mult).then_inc(s_rows, 1)

            dve.wait_ge(s_zero, NQ + 1)
            dve.wait_ge(s_base, 32)

            def add_h1(i):
                at = i * D
                b = seq1[:, bass.ds(at, D)]
                nc.vector.tensor_tensor(b, b, seq0[:, bass.ds(at, D)], ALU.add)

            groups(dve, layer_group(1), add_h1)

            for q in range(NQ + 2):
                if q < NQ:
                    inverse(1, q)
                    for j in range(quad(q)):
                        last = nc.vector.scalar_tensor_tensor(
                            out=base_rows[:, 4 * q + j, :], in0=bank[q % 2][:, j * P:(j + 1) * P],
                            scalar=rinv[:, q % 2, j:j + 1], in1=base_rows[:, 4 * q + j, :],
                            op0=ALU.mult, op1=ALU.add)
                    last.then_inc(s_rows, 1)
                if q >= 2:
                    r = q - 2
                    w = quad(r)
                    dve.wait_ge(s_g1, r + 1)
                    if r >= 2:
                        dve.wait_ge(s_gst[r % 2], 16 * (r // 2))
                    nc.vector.tensor_scalar(g1_out[:, r % 2, 0:w, :],
                                            bank[6 + r % 2][:, 0:w * D].rearrange("p (j d) -> p j d", j=w),
                                            1.0 / (LAYERS + 1), None, ALU.mult).then_inc(s_g1c, 1)

            def norm_columns(q, par, w):
                dve.wait_ge(s_nroot, q + 1)
                r = root[:, par, 0:w]
                at = bass.ds(q * 512, w)
                nc.vector.tensor_scalar(r, r, 3 * EPS, None, ALU.max).then_inc(s_nclip, 1)
                dve.wait_ge(s_nclip, q * 2 + 1)
                nc.vector.reciprocal(r, r).then_inc(s_nclip, 1)
                dve.wait_ge(s_nclip, q * 2 + 2)
                nc.vector.tensor_tensor(sumT[:, at], sumT[:, at], r, ALU.mult).then_inc(s_gn, 1)

            with dve.Fori(0, NQ // 2) as v:
                norm_columns(v * 2, 0, 512)
                norm_columns(v * 2 + 1, 1, 512)
            norm_columns(NQ - 1, 0, quad(NQ - 1) * P)

            def step(s, par, half, A, B, C):
                u, uh = s - 2, half - 1
                m0 = s * NC - NC
                own, prev = seq[par], seq[1 - par]

                def sess_chunk(c):
                    dve.wait_ge(s_beta, m0 + (c + 1))
                    n = len(CH[c])
                    l0 = CH[c][0]
                    b = bm[:, c % 2, 0:n]
                    at = bass.ds(s * L + (l0 - L), n)
                    nc.vector.tensor_tensor(b, bank[4][:, (1 - par) * 64 + l0:(1 - par) * 64 + l0 + n],
                                            mask[:, at], ALU.mult).then_inc(s_bm, 1)
                    if not (isinstance(s, int) and s == 1 and c == 0):
                        dve.wait_ge(s_free, m0 + c)
                    dve.wait_ge(s_bm, m0 + (c + 1))
                    for i, l in enumerate(CH[c]):
                        acc, w = sess_acc[:, i, :], bm[:, c % 2, i:i + 1]
                        if c == 0:
                            last = nc.vector.tensor_scalar(acc, prev[:, l, 0:D], w, None, ALU.mult)
                        else:
                            last = nc.vector.scalar_tensor_tensor(out=acc, in0=prev[:, l, 0:D], scalar=w,
                                                                  in1=acc, op0=ALU.mult, op1=ALU.add)
                    last.then_inc(s_free, 1)

                for c in range(NC):
                    if B:
                        n = len(CH[c])
                        slot = (par + 1 + c) % 2
                        dve.wait_ge(s_mm2, m0 + (c + 1))
                        if c == 0:
                            dve.wait_ge(s_qT, s)
                        if not (isinstance(s, int) and s == 1 and c < 2):
                            dve.wait_ge(s_beta, m0 + (c - 1))
                        nc.vector.tensor_tensor(
                            two[:, slot, 0:n * P].rearrange("p (i b) -> p i b", i=n),
                            bank[2 + slot][:, 0:n * P].rearrange("p (i b) -> p i b", i=n),
                            qT[:, :].unsqueeze(1).broadcast_to([P, n, P]), ALU.add).then_inc(s_qadd, 1)
                    if C and c < NS_D:
                        k = 2 * c + 1
                        j = k // BC
                        if k - 2 < BC * j:
                            n2 = (NB * par + j) // 2
                            if not (isinstance(s, int) and uh * NB + n2 == 0):
                                dve.wait_ge(s_out[(par + j) % 2], uh * (16 * NB) + 16 * n2)
                        dve.wait_ge(s_score, u * NS + (k + 1))
                        nc.vector.tensor_copy(stage[:, (par + j) % 2, (k - BC * j) * SC:(k - BC * j + 1) * SC],
                                              bank[6][:, 0:SC]).then_inc(s_evD, 1)
                    if A:
                        full = 16 * len(CH[c])
                        dve.wait_ge(s_land[par][c], half * full + full)
                        if not (isinstance(s, int) and s == 0 and c == 0):
                            dve.wait_ge(s_hsum, s * NC + c)
                        for i, l in enumerate(CH[c]):
                            acc, mk = hs_acc[:, i, :], mask[:, bass.ds(s * L + l, 1)]
                            if c == 0:
                                last = nc.vector.tensor_scalar(acc, own[:, l, 0:D], mk, None, ALU.mult)
                            else:
                                last = nc.vector.scalar_tensor_tensor(out=acc, in0=own[:, l, 0:D], scalar=mk,
                                                                      in1=acc, op0=ALU.mult, op1=ALU.add)
                        last.then_inc(s_hsum, 1)
                    if B and c >= 1:
                        sess_chunk(c - 1)
                if A:
                    dve.wait_ge(s_hsum, s * NC + NC)
                    if not (isinstance(s, int) and s == 0):
                        dve.wait_ge(s_q, s)
                    nc.vector.tensor_reduce(hs_row[:, :], hs_acc[:, :, :].rearrange("p a d -> p d a"), AX_X,
                                            ALU.add).then_inc(s_hred, 1)
                    dve.wait_ge(s_hred, s + 1)
                    nc.vector.tensor_scalar(hs_row[:, :], hs_row[:, :], rcnt3[:, bass.ds(s, 1)], None,
                                            ALU.mult).then_inc(s_hs, 1)
                if B:
                    row = selT[:, 1 - par, :]
                    sess_chunk(NC - 1)
                    dve.wait_ge(s_free, s * NC)
                    nc.vector.tensor_reduce(row, sess_acc[:, :, :].rearrange("p a d -> p d a"), AX_X,
                                            ALU.add).then_inc(s_sred, 1)
                    dve.wait_ge(s_sred, s * 3 - 2)
                    nc.vector.tensor_tensor_reduce(out=two[:, 0, 0:D], in0=row, in1=row,
                                                   scale=1.0, scalar=0.0, op0=ALU.mult, op1=ALU.add,
                                                   accum_out=small[:, 0:1]).then_inc(s_n2, 1)
                    dve.wait_ge(s_nn, s)
                    nc.vector.tensor_scalar(small[:, 2:3], small[:, 1:2], 3 * EPS, None,
                                            ALU.max).then_inc(s_sred, 1)
                    dve.wait_ge(s_sred, s * 3 - 1)
                    nc.vector.reciprocal(small[:, 3:4], small[:, 2:3]).then_inc(s_sred, 1)
                    dve.wait_ge(s_sred, s * 3)
                    nc.vector.tensor_scalar(row, row, small[:, 3:4], W_K, ALU.mult, ALU.mult).then_inc(s_sel, 1)

            session_steps(dve, step)

        @block.tensor
        def _(pe):
            pe.wait_ge(s_const, 3)
            n = 0
            for q, x, s, v in ((0, col_f, s_colf, 4), (1, row_f, s_rel, 2), (2, val_f, s_val, 48)):
                pe.wait_ge(s, v)
                for h in range(2):
                    for jj in range(2):
                        if n >= 4:
                            pe.wait_ge(s_tab, n - 3)
                        for j in range(4):
                            at = (4 * jj + j) * P
                            last = nc.tensor.transpose(bank[n % 4][:, j * HG:(j + 1) * HG],
                                                       x[:, h, at:at + P], ident[0:HG, 0:HG])
                        last.then_inc(s_tab_t, 1)
                        n += 1
            pe.wait_ge(s_rel, 3)
            for h in range(2):
                for k in range(2):
                    last = nc.tensor.transpose(bank[4][0:1, (2 * h + k) * HG:(2 * h + k + 1) * HG],
                                               sched_f[:, h, k:k + 1], ident[0:HG, 0:HG])
            last.then_inc(s_sched_t, 1)
            pe.wait_ge(s_w, 16 * 7)
            nc.tensor.transpose(bank[5][:, 0:L], pos_sb[0:L, :], ident[0:L, 0:L])
            nc.tensor.transpose(bank[6][:, 0:D], glu1_sb, ident[:, :])
            nc.tensor.transpose(bank[6][:, D:2 * D], glu2_sb, ident[:, :]).then_inc(s_w_t, 1)
            pe.wait_ge(s_w_c, 3)
            nc.tensor.matmul(bank[7][:, 0:L], w1a, hsT[:, 0:L], start=True, stop=True).then_inc(s_w_t, 1)

            pe.wait_ge(s_sched, 1)
            pe.wait_ge(s_tab, 12)
            pe.wait_ge(s_ones, 1)
            rounds = pe.alloc_register("pe_rounds")
            n_rounds = pe.alloc_register("pe_n_rounds")
            pe.reg_mov(rounds, 0)
            for layer in range(LAYERS):
                def sum_group(g, i, slot, tiles):
                    pe.reg_load(n_rounds, sched[0:1, bass.ds(g * 2, 1)])
                    done = layer * (SLOT0 if slot == 0 else SLOT1)
                    with pe.Fori(0, n_rounds):
                        pe.reg_add(rounds, rounds, 1)
                        pe.wait_ge(s_gath[slot], i * (TG * 16) + (tiles * 16 + done))
                        pe.wait_ge(s_onehot, rounds)
                        for j in range(tiles):
                            last = nc.tensor.matmul(bank[0][:, 0:P], gath[:, slot, j, :], onehot[:, j, :],
                                                    start=(j == 0), stop=(j == tiles - 1))
                        last.then_inc(s_window, 1)

                groups(pe, sum_group)

                pe.wait_ge(s_group, (layer + 1) * NG + 2)
                for q in range(NQ + 2):
                    if q < NQ:
                        if q >= 2:
                            pe.wait_ge(s_rows, layer * NQ + q - 1)
                        for j in range(quad(q)):
                            at = 512 * q + j * P
                            nc.tensor.transpose(bank[q % 2][:, j * P:(j + 1) * P], sumT[:, at:at + P], ident[:, :])
                        pe.wait_ge(s_sq, layer * NQ + q + 1)
                        for j in range(quad(q)):
                            last = nc.tensor.matmul(bank[2 + q % 2][:, j:j + 1], two[:, q % 2, j * P:(j + 1) * P],
                                                    ones[:, 0:1], start=True, stop=True)
                        last.then_inc(s_fin, 1)
                    if layer == 1 and 1 <= q <= NQ:
                        r = q - 1
                        pe.wait_ge(s_rows, NQ + r + 1)
                        if r >= 2:
                            pe.wait_ge(s_gtc, r - 1)
                        for j in range(quad(r)):
                            last = nc.tensor.transpose(bank[4 + r % 2][:, j * P:(j + 1) * P],
                                                       base_rows[:, 4 * r + j, :], ident[:, :])
                        last.then_inc(s_gt, 1)
                    if layer == 1 and q >= 2:
                        r = q - 2
                        pe.wait_ge(s_gtc, r + 1)
                        if r >= 2:
                            pe.wait_ge(s_g1c, r - 1)
                        for j in range(quad(r)):
                            at = 512 * r + j * P
                            last = nc.tensor.matmul(bank[6 + r % 2][:, j * D:(j + 1) * D], sumT[:, at:at + P],
                                                    w1b, start=True, stop=True)
                        last.then_inc(s_g1, 1)

            def norm_sums(q, par, w, first):
                pe.wait_ge(s_nsq, q + 1)
                if not first:
                    pe.wait_ge(s_nroot, q - 1)
                nc.tensor.matmul(bank[par][:, 0:w], ones, two[:, par, 0:w], start=True, stop=True).then_inc(s_nsum, 1)

            norm_sums(0, 0, 512, True)
            norm_sums(1, 1, 512, True)
            with pe.Fori(1, NQ // 2) as v:
                norm_sums(v * 2, 0, 512, False)
                norm_sums(v * 2 + 1, 1, 512, False)
            norm_sums(NQ - 1, 0, quad(NQ - 1) * P, False)
            pe.wait_ge(s_nroot, NQ)

            def step(s, par, half, A, B, C):
                u = s - 2
                m0 = s * NC - NC

                def betas(c):
                    slot = (par + 1 + c) % 2
                    pe.wait_ge(s_sig, m0 + (c + 1))
                    if not (isinstance(s, int) and s == 1 and c == 0):
                        pe.wait_ge(s_bm, m0 + c)
                    for i, l in enumerate(CH[c]):
                        last = nc.tensor.matmul(bank[4][:, (1 - par) * 64 + l:(1 - par) * 64 + l + 1],
                                                two[:, slot, i * P:(i + 1) * P], w2c[:, :], start=True, stop=True)
                    last.then_inc(s_beta, 1)

                def scores(k):
                    if not (isinstance(s, int) and s == 2 and k < 2):
                        if k % 2 == 0:
                            pe.wait_ge(s_evA, u * NS_A + k // 2)
                        else:
                            pe.wait_ge(s_evD, u * NS_D + k // 2)
                    nc.tensor.matmul(bank[5 + k % 2][:, 0:SC], selT[:, par, :], sumT[:, k * SC:(k + 1) * SC],
                                     start=True, stop=True).then_inc(s_score, 1)

                if C:
                    pe.wait_ge(s_selT, s - 1)
                for c in range(NC):
                    if B:
                        slot = (par + 1 + c) % 2
                        w = len(CH[c]) * P
                        pe.wait_ge(s_tanh, m0 + (c + 1))
                        if not (isinstance(s, int) and s == 1 and c < 2):
                            pe.wait_ge(s_qadd, m0 + (c - 1))
                        nc.tensor.matmul(bank[2 + slot][:, 0:w], glu1T[:, :], nh[:, c, 0:w],
                                         start=True, stop=True).then_inc(s_mm2, 1)
                    if C:
                        scores(2 * c)
                        if 2 * c + 1 < NS:
                            scores(2 * c + 1)
                    if B and c >= 1:
                        betas(c - 1)
                    if A:
                        full = 16 * len(CH[c])
                        pe.wait_ge(s_land[par][c], half * full + full)
                        if not (isinstance(s, int) and s == 0 and c < 2):
                            pe.wait_ge(s_tanh, s * NC + (c - 1))
                        for i, l in enumerate(CH[c]):
                            last = nc.tensor.transpose(bank[(par + c) % 2][:, i * P:(i + 1) * P],
                                                       seq[par][:, l, D:2 * D], ident[:, :])
                        last.then_inc(s_g1t, 1)
                if B:
                    betas(NC - 1)
                if A:
                    pe.wait_ge(s_hs, s + 1)
                    nc.tensor.transpose(bank[7][:, 0:P], hs_row[:, :], ident[:, :]).then_inc(s_hst, 1)
                    pe.wait_ge(s_hsT, s + 1)
                    nc.tensor.matmul(bank[7][:, P:2 * P], glu2T[:, :], hsT[:, :], start=True,
                                     stop=True).then_inc(s_q, 1)
                if B:
                    pe.wait_ge(s_sel, s)
                    if A:
                        pe.wait_ge(s_qT, s + 1)
                    nc.tensor.transpose(bank[7][:, 2 * P:3 * P], selT[:, 1 - par, :], ident[:, :]).then_inc(s_selt, 1)

            session_steps(pe, step)


_INS = ['r_items', 'r_inputs', 'r_alias_inputs', 'L0_rec_adj_row', 'L0_rec_adj_col', 'L0_rec_adj_val', 'L0_rec_E',
        'L0_rec_pos_emb', 'L0_rec_w1', 'L0_rec_w2', 'L0_rec_glu1_w', 'L0_rec_glu1_b', 'L0_rec_glu2_w']


def kernel(**inputs):
    import numpy as _np
    import concourse.bacc as _bacc
    from concourse import mybir as _mybir
    from concourse.bass_utils import run_bass_kernel_spmd as _run

    nc = _bacc.Bacc("TRN2", target_bir_lowering=False, num_devices=1)
    arrays, args = {}, []
    for name in _INS:
        a = _np.ascontiguousarray(inputs[name])
        arrays[f"in_{name}_dram"] = a
        args.append(nc.dram_tensor(f"in_{name}_dram", a.shape, _mybir.dt.from_np(a.dtype), kind="ExternalInput").ap())
    shape = (inputs['r_items'].shape[0], inputs['L0_rec_E'].shape[0])
    args.append(nc.dram_tensor("out_0_dram", shape, _mybir.dt.float32, kind="ExternalOutput").ap())
    build(nc, *args)
    r = _run(nc, [arrays], core_ids=[0])
    return r.results[0]["out_0_dram"]
```

```python
from contextlib import ExitStack

import concourse.bass as bass
from concourse import mybir

F32 = mybir.dt.float32
I32 = mybir.dt.int32
U32 = mybir.dt.uint32
ALU = mybir.AluOpType
ACT = mybir.ActivationFunctionType
AX_X = mybir.AxisListType.X

P = 128
EPS = 1e-12
W_K = 12.0
LAYERS = 2
FAR = 1e10


def build(nc, items, inputs, alias, adj_row, adj_col, adj_val, E, pos_emb, w1, w2,
          glu1_w, glu1_b, glu2_w, out):
    N, D = E.shape
    S, L = items.shape
    NNZ = adj_row.shape[0]
    assert D == P and S % P == 0 and L <= P

    TG = 8
    EG = TG * P
    NG = -(-NNZ // EG)
    HG = NG // 2
    TAIL = NNZ - (NG - 1) * EG
    TAIL_T = -(-TAIL // P)
    PAIRS = NG // 2 - 1
    assert NG == 2 * HG and HG <= P

    NT = -(-N // P)
    NQ = -(-NT // 4)
    NP_ = NT * P
    LAST_T = N - (NT - 1) * P
    assert NT == PAIRS + 1 and NT <= L * 2

    def quad(q):
        return min(4, NT - 4 * q)

    T = S // P
    CH = [list(range(4 * c, min(4 * c + 4, L))) for c in range(-(-L // 4))]
    NC = len(CH)
    assert T % 2 == 0 and NC % 2 == 1
    IDX_L = 5
    IDX_C = L // IDX_L

    SC = 500
    NS = N // SC
    BC = 3
    NB = -(-NS // BC)
    assert NS * SC == N and NS % 2 == 1 and NB % 2 == 1
    SCORE_AT = 5
    NS_A, NS_D = (NS + 1) // 2, NS // 2

    h1_dram = nc.dram_tensor("h1_rows", (NP_, D), F32).ap()
    graph_dram = nc.dram_tensor("graph_rows", (NP_, 2 * D), F32).ap()

    with ExitStack() as ctx:
        def sb(name, shape, dt=F32):
            return ctx.enter_context(nc.sbuf_tensor(name, shape, dt))

        def sem(name):
            return ctx.enter_context(nc.semaphore(name))

        sumT = sb("sumT", [P, N + P])
        seq0 = sb("seq0", [P, L * 2 * D])
        seq1 = sb("seq1", [P, L * 2 * D])
        seq = [x[:, :].rearrange("p (l d) -> p l d", l=L) for x in (seq0, seq1)]
        h1_rows = seq0[:, 0:NT * D].rearrange("p (t d) -> p t d", d=D)
        base_rows = seq1[:, 0:NT * D].rearrange("p (t d) -> p t d", d=D)

        def raw(n, dt=F32):
            v = seq0[0:HG, 2 * EG * n:2 * EG * (n + 1)]
            return (v if dt is F32 else v.bitcast(dt)).rearrange("g (h n) -> g h n", h=2)

        row_i, col_i, val_f = raw(0, I32), raw(1, I32), raw(2)
        row_f, tmp_f, col_f = raw(3), raw(4), raw(5)

        work = sb("work", [P, 3 * TG * NG + 2 * TG * D])
        table = work[:, 0:3 * TG * NG].rearrange("p (q g) -> p q g", g=NG)
        gath = work[:, 3 * TG * NG:].rearrange("p (s j d) -> p s j d", s=2, j=TG)
        nh = work[:, 0:NC * 4 * P].rearrange("p (c n) -> p c n", c=NC)

        onehot_b = sb("onehot", [P, TG * P])
        onehot = onehot_b[:, :].rearrange("p (j r) -> p j r", j=TG)
        two = onehot_b[:, :].rearrange("p (s n) -> p s n", s=2)

        stage_b = sb("stage", [P, 2 * BC * SC])
        stage = stage_b[:, :].rearrange("p (s n) -> p s n", s=2)
        items_i = stage_b[:, 0:T * L].bitcast(I32)
        alias_i = stage_b[:, T * L:2 * T * L].bitcast(I32)
        inputs_i = stage_b[:, 2 * T * L:3 * T * L].bitcast(I32)
        pick = stage_b[:, 3 * T * L:3 * T * L + IDX_L * L].rearrange("p (l m) -> p l m", l=IDX_L)
        squares = stage_b[:, 0:4 * 4 * P].rearrange("p (s n) -> p s n", s=4)
        g1_out = two.rearrange("p s (j d) -> p s j d", j=4)

        item_idx = sb("item_idx", [P, (T + 1) * L], U32)
        mask = sb("mask", [P, T * L])
        ident = sb("ident", [P, P])
        glu1T = sb("glu1T", [P, D])
        glu2T = sb("glu2T", [P, D])
        posT = sb("posT", [P, L])
        w2c = sb("w2c", [P, 1])
        b1c = sb("b1c", [P, 1])
        hs_acc = sb("hs_acc", [P, 4, D])
        sess_acc = sb("sess_acc", [P, 4, D])
        hsT = sb("hsT", [P, P])
        qT = sb("qT", [P, P])
        selT = sb("selT", [P, 2, P])
        rcnt3 = sb("rcnt3", [P, T])
        bm = sb("bm", [P, 2, 4])
        small = sb("small", [P, 8])
        square_dump = sb("square_dump", [P, D])
        rinv = sb("rinv", [P, NT])
        idx_l = sb("idx_l", [P, 2, IDX_L])
        idx_slot = sb("idx_slot", [P, 2, TG], U32)
        edge_slot = sb("edge_slot", [P, 2, 2 * TG])
        sess_idx = sb("sess_idx", [P, 2, L], U32)
        sched_f = sb("sched_f", [HG, 2, 2])
        sched_i = sb("sched_i", [HG, 2], I32)
        iota = qT
        w1b = selT[:, 0, :]
        ones = selT[:, 1, :]
        sched = hs_acc[0:1, :, :].rearrange("o a b -> o (a b)")[:, 0:2 * NG].bitcast(I32)
        pos_sb, glu1_sb, glu2_sb, w1a = (sess_acc[:, i, :] for i in range(4))
        hs_row = hsT

        bank = [ctx.enter_context(nc.psum_tensor(f"bank{b}", [P, 512], F32)) for b in range(8)]

        s_pad = sem("s_pad")
        s_row, s_col, s_val = sem("s_row"), sem("s_col"), sem("s_val")
        s_w = sem("s_w")
        s_sess_in = sem("s_sess_in")
        s_base = sem("s_base")
        s_const = sem("s_const")
        s_ones = sem("s_ones")
        s_colf = sem("s_colf")
        s_rel = sem("s_rel")
        s_tab_t = sem("s_tab_t")
        s_tab = sem("s_tab")
        s_sched_t, s_sched = sem("s_sched_t"), sem("s_sched")
        s_w_t, s_w_c = sem("s_w_t"), sem("s_w_c")
        s_mask = sem("s_mask")
        s_gidx = sem("s_gidx")
        s_edge = sem("s_edge")
        s_gath = [[sem(f"s_gath{i}_{j}") for j in range(TG)] for i in range(2)]
        s_onehot = sem("s_onehot")
        s_window = sem("s_window")
        s_group = sem("s_group")
        s_sqA, s_sqD = sem("s_sqA"), sem("s_sqD")
        s_ssq = sem("s_ssq")
        s_norm = sem("s_norm")
        s_rinv = sem("s_rinv")
        s_rowT = sem("s_rowT")
        s_rowsA, s_rowsD = sem("s_rowsA"), sem("s_rowsD")
        s_h1 = sem("s_h1")
        s_zero = sem("s_zero")
        s_gt, s_gtc = sem("s_gt"), sem("s_gtc")
        s_g1, s_g1c = sem("s_g1"), sem("s_g1c")
        s_gst = [sem("s_gst0"), sem("s_gst1")]
        s_gr = sem("s_gr")
        s_nsq, s_nsum = sem("s_nsq"), sem("s_nsum")
        s_nroot, s_gn = sem("s_nroot"), sem("s_gn")
        s_sidx_pad = sem("s_sidx_pad")
        s_sidx = sem("s_sidx")
        s_land = [[sem(f"s_land{i}_{c}") for c in range(NC)] for i in range(2)]
        s_g1t = sem("s_g1t")
        s_tanh = sem("s_tanh")
        s_mm2, s_qadd, s_sig = sem("s_mm2"), sem("s_qadd"), sem("s_sig")
        s_beta = sem("s_beta")
        s_free = sem("s_free")
        s_link, s_dec, s_pick = sem("s_link"), sem("s_dec"), sem("s_pick")
        s_bm, s_hsum, s_hred, s_sred = (sem(x) for x in ("s_bm", "s_hsum", "s_hred", "s_sred"))
        s_hs, s_hst, s_hsT, s_q, s_qT = (sem(x) for x in ("s_hs", "s_hst", "s_hsT", "s_q", "s_qT"))
        s_n2, s_nn, s_sel, s_selt, s_selT = (sem(x) for x in ("s_n2", "s_nn", "s_sel", "s_selt", "s_selT"))
        s_score = sem("s_score")
        s_evA, s_evD = sem("s_evA"), sem("s_evD")
        s_pool, s_sp = sem("s_pool"), sem("s_sp")
        s_out = [sem("s_out0"), sem("s_out1")]

        def edges(x, half):
            if half == 0:
                return x[0:HG * EG].rearrange("(g n) -> g n", n=EG)
            return x[HG * EG:(NG - 1) * EG].rearrange("(g n) -> g n", n=EG)

        def by_tile(x):
            return x.rearrange("(p t) l -> p (t l)", t=T)

        graph_v = graph_dram.rearrange("(t p) c -> p t c", p=P)
        h1_v = h1_dram.rearrange("(t p) c -> p t c", p=P)
        out_v = out.rearrange("(p t) n -> p t n", t=T)

        def landed(layer, i, slot, j):
            per_layer = HG - (slot == 1 and j >= TAIL_T)
            return i * 16 + 16 * (1 + layer * per_layer)

        def rows_by(layer, q):
            n_a = NQ // 4
            if layer == 0:
                if q % 4 == 3:
                    return s_rowsA, q // 4 + 1
                return s_rowsD, q + 1 - (q + 1) // 4
            return s_rowsD, NQ - n_a + q + 1

        def squared(layer, q):
            if q % 2 == 0:
                return s_sqA, layer * ((NQ + 1) // 2) + q // 2 + 1
            return s_sqD, layer * (NQ // 2) + q // 2 + 1

        def groups(eng, body, pair_extra=None, start=0):
            with eng.Fori(start, PAIRS) as i:
                body(i * 2, i, 0, TG)
                body(i * 2 + 1, i, 1, TG)
                if pair_extra is not None:
                    pair_extra(i)
            body(NG - 2, PAIRS, 0, TG)
            body(NG - 1, PAIRS, 1, TAIL_T)
            if pair_extra is not None:
                pair_extra(PAIRS)

        def session_steps(step, eng):
            for s in range(4):
                step(s, s % 2, s // 2)
            with eng.Fori(2, T // 2) as v:
                step(v * 2, 0, v)
                step(v * 2 + 1, 1, v)
            for s in range(T, T + 3):
                step(s, s % 2, s // 2)

        def have(s, back):
            return not isinstance(s, int) or 0 <= s - back < T

        def lagged(par, c, lag):
            if c >= lag:
                return 1, 1 - par, c - lag
            return 2, par, c - lag + NC

        def score_slot(par, half, c):
            if c >= SCORE_AT:
                k = 2 * (c - SCORE_AT)
                return 2, par, half - 1, [k, k + 1]
            k = 2 * (c - SCORE_AT + NC)
            return 3, 1 - par, half - 2 + par, [x for x in (k, k + 1) if x < NS]

        block = ctx.enter_context(nc.Block())

        @block.sync
        def _(sp):
            for x, dst, s in ((adj_col, col_i, s_col), (adj_row, row_i, s_row), (adj_val, val_f, s_val)):
                sp.dma_start(dst[:, 0, :], edges(x, 0)).then_inc(s, 16)
                if x is adj_col:
                    sp.wait_ge(s_pad, 3)
                sp.dma_start(dst[0:HG - 1, 1, :], edges(x, 1)).then_inc(s, 16)
                sp.dma_start(dst[HG - 1:HG, 1, 0:TAIL],
                             x[(NG - 1) * EG:NNZ].rearrange("(g n) -> g n", g=1)).then_inc(s, 16)
            for dst, src in ((w1a, w1[0:D, :]), (w1b, w1[D:2 * D, :]), (pos_sb[0:L, :], pos_emb),
                             (glu1_sb, glu1_w), (glu2_sb, glu2_w), (w2c[:, :], w2),
                             (b1c[:, :], glu1_b.rearrange("(p o) -> p o", o=1))):
                sp.dma_start(dst, src).then_inc(s_w, 16)
            for dst, src in ((items_i, items), (alias_i, alias), (inputs_i, inputs)):
                sp.dma_start(dst, by_tile(src)).then_inc(s_sess_in, 16)
            sp.wait_ge(s_pad, 4)
            sp.dma_start(base_rows[:, 0:NT - 1, :],
                         E[0:(NT - 1) * P, :].rearrange("(t p) d -> p t d", p=P)).then_inc(s_base, 16)
            sp.dma_start(base_rows[0:LAST_T, NT - 1, :], E[(NT - 1) * P:N, :]).then_inc(s_base, 16)

            for q in range(NQ):
                sp.wait_ge(*rows_by(0, q))
                sp.dma_start(h1_v[:, 4 * q:4 * q + quad(q), :],
                             h1_rows[:, 4 * q:4 * q + quad(q), :]).then_inc(s_h1, 16)
            for q in range(NQ):
                t0, t1 = 4 * q, 4 * q + quad(q)
                sp.wait_ge(*rows_by(1, q))
                sp.dma_start(graph_v[:, t0:t1, 0:D], base_rows[:, t0:t1, :]).then_inc(s_gr, 16)
                sp.wait_ge(s_g1c, q + 1)
                sp.dma_start(graph_v[:, t0:t1, D:2 * D],
                             g1_out[:, q % 2, 0:quad(q), :]).then_inc(s_gst[q % 2], 16)

            def store_tile(u, par):
                for j in range(NB):
                    end = min(BC * (j + 1), NS)
                    sp.wait_ge(s_evA, u * NS_A + (end + 1) // 2)
                    sp.sem_inc(s_sp, 1)
                    sp.wait_ge(s_evD, u * NS_D + end // 2)
                    sp.sem_inc(s_sp, 1)
                    slot = (par + j) % 2
                    sp.dma_start(out_v[:, bass.ds(u, 1), BC * SC * j:SC * end],
                                 stage[:, slot:slot + 1, 0:SC * end - BC * SC * j]).then_inc(s_out[slot], 16)

            with sp.Fori(0, T // 2) as v:
                store_tile(v * 2, 0)
                store_tile(v * 2 + 1, 1)
            sp.wait_ge(s_out[0], 16 * (T * NB // 2))
            sp.wait_ge(s_out[1], 16 * (T * NB // 2))

        @block.gpsimd
        def _(pool):
            nc.gpsimd.iota(iota[:, :], [[1, P]], base=0, channel_multiplier=0,
                           allow_small_or_imprecise_dtypes=True).then_inc(s_const, 1)
            nc.gpsimd.iota(ident[:, :], [[1, P]], base=0, channel_multiplier=-1,
                           allow_small_or_imprecise_dtypes=True).then_inc(s_const, 1)
            pool.wait_ge(s_const, 2)
            nc.gpsimd.tensor_scalar(ident[:, :], ident[:, :], 0.0, None, ALU.is_equal).then_inc(s_const, 1)
            pool.wait_ge(s_const, 3)
            nc.gpsimd.memset(item_idx[:, T * L:(T + 1) * L], 0).then_inc(s_sidx_pad, 1)
            nc.gpsimd.memset(sumT[:, :], 0.0).then_inc(s_zero, 1)

            for layer in range(LAYERS):
                src = E if layer == 0 else h1_dram
                if layer == 1:
                    for q in range(NQ):
                        pool.wait_ge(s_rowT, q + 1)
                        end = 512 * (q + 1) if q < NQ - 1 else N + P
                        nc.gpsimd.memset(sumT[:, 512 * q:end], 0.0).then_inc(s_zero, 1)
                    pool.wait_ge(s_h1, 16 * NQ)

                def gather(g, i, slot, tiles):
                    pool.wait_ge(s_gidx, g + (layer * NG + 1))
                    pool.sem_inc(s_pool, 1)
                    for j in range(tiles):
                        nc.gpsimd.indirect_dma_start(
                            out=gath[:, slot, j, :], out_offset=None, in_=src,
                            in_offset=bass.IndirectOffsetOnAxis(ap=idx_slot[:, slot, j:j + 1], axis=0),
                        ).then_inc(s_gath[slot][j], 16)

                groups(pool, gather)

            pool.wait_ge(s_gr, 16 * NQ)
            pool.wait_ge(s_gst[0], 16 * ((NQ + 1) // 2))
            pool.wait_ge(s_gst[1], 16 * (NQ // 2))

            def step(s, par, half):
                if not have(s, 0):
                    return
                pool.wait_ge(s_sidx, s + 1)
                pool.sem_inc(s_pool, 1)
                for c in range(NC):
                    if have(s, 2):
                        pool.wait_ge(s_free, s * NC + (c + 1 - 2 * NC))
                        pool.sem_inc(s_pool, 1)
                    for l in CH[c]:
                        nc.gpsimd.indirect_dma_start(
                            out=seq[par][:, l, :], out_offset=None, in_=graph_dram,
                            in_offset=bass.IndirectOffsetOnAxis(ap=sess_idx[:, par, l:l + 1], axis=0),
                        ).then_inc(s_land[par][c], 16)

            session_steps(step, pool)

        @block.scalar
        def _(act):
            def copy_table(n):
                q, h, jj = n // 4, n // 2 % 2, n % 2
                act.wait_ge(s_tab_t, n + 1)
                nc.scalar.copy(table[:, q * TG + 4 * jj:q * TG + 4 * jj + 4, h * HG:(h + 1) * HG],
                               bank[n % 4][:, 0:4 * HG].rearrange("p (j g) -> p j g", j=4)).then_inc(s_tab, 1)

            def stage_indices(g, slot):
                nc.scalar.copy(idx_slot[:, slot, :], table[:, 0:TG, bass.ds(g, 1)]
                               .rearrange("p q o -> p (q o)")).then_inc(s_gidx, 1)

            def stage_edges(g, slot):
                nc.scalar.copy(edge_slot[:, slot, :], table[:, TG:3 * TG, bass.ds(g, 1)]
                               .rearrange("p q o -> p (q o)")).then_inc(s_edge, 1)

            for n in range(4):
                copy_table(n)
            act.wait_ge(s_tab, 4)
            for g in range(2):
                stage_indices(g, g)
            for n in range(4, 12):
                copy_table(n)
            act.wait_ge(s_tab, 12)
            for g in range(2):
                stage_edges(g, g)
            act.wait_ge(s_sched_t, 1)
            nc.scalar.copy(sched.rearrange("o (h g k) -> o h k g", h=2, k=2),
                           bank[4][0:1, 0:4 * HG].rearrange("o (h k g) -> o h k g", h=2, k=2)).then_inc(s_sched, 1)
            act.wait_ge(s_w_t, 1)
            nc.scalar.copy(hsT[:, 0:L], bank[5][:, 0:L]).then_inc(s_w_c, 1)
            nc.scalar.copy(glu1T[:, :], bank[6][:, 0:D]).then_inc(s_w_c, 1)
            nc.scalar.copy(glu2T[:, :], bank[6][:, D:2 * D]).then_inc(s_w_c, 1)
            act.wait_ge(s_w_t, 2)
            nc.scalar.copy(posT[:, :], bank[7][:, 0:L]).then_inc(s_w_c, 1)

            for layer in range(LAYERS):
                def stage_group(g, i, slot, tiles):
                    act.wait_ge(s_group, g + (layer * NG + 1))
                    stage_indices(g, slot)
                    stage_edges(g, slot)

                groups(act, stage_group, start=1 - layer)

                act.wait_ge(s_group, (layer + 1) * NG + 2)
                for q in range(0, NQ, 2):
                    if q >= 4:
                        act.wait_ge(s_ssq, layer * NQ + q - 3)
                    w = quad(q) * P
                    nc.scalar.activation(squares[:, q % 4, 0:w], sumT[:, 512 * q:512 * q + w],
                                         ACT.Square).then_inc(s_sqA, 1)
                act.wait_ge(s_ssq, (layer + 1) * NQ)
                nc.scalar.activation(rinv[:, :], bank[7][:, 0:NT], ACT.Sqrt).then_inc(s_norm, 1)
                if layer == 0:
                    act.wait_ge(s_rinv, 1)
                    for q in range(3, NQ, 4):
                        act.wait_ge(s_rowT, q + 1)
                        for j in range(quad(q)):
                            last = nc.scalar.activation(h1_rows[:, 4 * q + j, :], bank[q % 3][:, j * P:(j + 1) * P],
                                                        ACT.Copy, scale=rinv[:, 4 * q + j:4 * q + j + 1])
                        last.then_inc(s_rowsA, 1)
                else:
                    for q in range(NQ + 1):
                        if q < NQ:
                            w = quad(q) * P
                            act.wait_ge(s_gt, q + 1)
                            nc.scalar.copy(sumT[:, 512 * q:512 * q + w], bank[3 + q % 2][:, 0:w]).then_inc(s_gtc, 1)
                        if q >= 1:
                            r = q - 1
                            w = quad(r)
                            act.wait_ge(s_g1, r + 1)
                            if r >= 2:
                                act.wait_ge(s_gst[r % 2], 16 * (r // 2))
                            nc.scalar.mul(g1_out[:, r % 2, 0:w, :],
                                          bank[5 + r % 2][:, 0:w * D].rearrange("p (j d) -> p j d", j=w),
                                          1.0 / (LAYERS + 1)).then_inc(s_g1c, 1)

            act.wait_ge(s_sidx_pad, 1)
            nc.scalar.copy(sess_idx[:, 0, :], item_idx[:, 0:L]).then_inc(s_sidx, 1)

            def norm_square(q):
                if q >= NQ:
                    return
                if q >= 2:
                    act.wait_ge(s_nsum, q - 1)
                w = quad(q) * P
                nc.scalar.activation(squares[:, q % 2, 0:w], sumT[:, 512 * q:512 * q + w], ACT.Square).then_inc(s_nsq, 1)

            norm_square(0)

            def step(s, par, half):
                if have(s, 0):
                    nc.scalar.copy(sess_idx[:, 1 - par, :],
                                   item_idx[:, bass.ds(s * L + L, L)]).then_inc(s_sidx, 1)
                for c in range(NC):
                    if isinstance(s, int) and s * NC + c < NQ:
                        q = s * NC + c
                        w = quad(q) * P
                        norm_square(q + 1)
                        act.wait_ge(s_nsum, q + 1)
                        if q >= 2:
                            act.wait_ge(s_gn, q - 1)
                        nc.scalar.activation(squares[:, 2 + q % 2, 0:w], bank[5 + q % 2][:, 0:w],
                                             ACT.Sqrt).then_inc(s_nroot, 1)
                    if c == 2 and have(s, 2):
                        act.wait_ge(s_n2, s - 1)
                        nc.scalar.activation(small[:, 1:2], small[:, 0:1], ACT.Sqrt).then_inc(s_nn, 1)
                    back, tp, ch = lagged(par, c, 1)
                    if have(s, back):
                        w = len(CH[ch]) * P
                        b = (par + c) % 2
                        act.wait_ge(s_qadd, s * NC + (c - NC))
                        nc.scalar.activation(two[:, b, 0:w], two[:, b, 0:w], ACT.Sigmoid).then_inc(s_sig, 1)
                    if c == 0 and have(s, 1):
                        act.wait_ge(s_hst, s)
                        nc.scalar.copy(hsT[:, :], bank[7][:, 0:P]).then_inc(s_hsT, 1)
                        act.wait_ge(s_q, s)
                        nc.scalar.activation(qT[:, :], bank[7][:, P:2 * P], ACT.Identity,
                                             bias=b1c[:, 0:1]).then_inc(s_qT, 1)
                    if c == 4 and have(s, 2):
                        act.wait_ge(s_selt, s - 1)
                        nc.scalar.copy(selT[:, par, :], bank[7][:, 2 * P:3 * P]).then_inc(s_selT, 1)
                    back, tp, uh, ks = score_slot(par, half, c)
                    if have(s, back):
                        k = ks[0]
                        j = k // BC
                        if k - 2 < BC * j:
                            n2 = (NB * tp + j) // 2
                            if not (isinstance(s, int) and uh * NB + n2 == 0):
                                act.wait_ge(s_out[(tp + j) % 2], uh * (16 * NB) + 16 * n2)
                        act.wait_ge(s_score, s * NS + (k + 1 - back * NS))
                        nc.scalar.copy(stage[:, (tp + j) % 2, (k - BC * j) * SC:(k - BC * j + 1) * SC],
                                       bank[5][:, 0:SC]).then_inc(s_evA, 1)
                    if have(s, 0):
                        act.wait_ge(s_g1t, s * NC + (c + 1))
                        if have(s, 1):
                            act.wait_ge(s_mm2, s * NC + (c + 1 - NC))
                        for i, l in enumerate(CH[c]):
                            last = nc.scalar.activation(nh[:, c, i * P:(i + 1) * P],
                                                        bank[(par + c) % 2][:, i * P:(i + 1) * P], ACT.Tanh,
                                                        bias=posT[:, L - 1 - l:L - l])
                        last.then_inc(s_tanh, 1)

            session_steps(step, act)

        @block.vector
        def _(dve):
            last = slice((HG - 1) // 32 * 32, HG)
            nc.vector.memset(row_i[last, 1, :], N).then_inc(s_pad, 1)
            nc.vector.memset(col_i[last, 1, :], 0).then_inc(s_pad, 1)
            nc.vector.memset(val_f[last, 1, :], 0.0).then_inc(s_pad, 1)
            nc.vector.memset(base_rows[:, NT - 1, :], 0.0).then_inc(s_pad, 1)
            nc.vector.memset(ones, 1.0).then_inc(s_ones, 1)
            chain = [0]

            def link(ins):
                chain[0] += 1
                ins.then_inc(s_link, 1)
                dve.wait_ge(s_link, chain[0])

            nc.vector.memset(small[:, 7:8], 0.0).then_inc(s_group, 2)
            dve.wait_ge(s_col, 48)
            link(nc.vector.tensor_scalar(tmp_f, col_i, 0.0, float(N), ALU.is_lt, ALU.mult))
            link(nc.vector.tensor_tensor(col_f, tmp_f, col_i, ALU.add))
            nc.vector.tensor_scalar(col_f, col_f, 0.0, float(N - 1), ALU.max, ALU.min).then_inc(s_colf, 1)
            dve.wait_ge(s_row, 48)
            link(nc.vector.tensor_scalar(tmp_f, row_i, 0.0, None, ALU.is_lt))
            link(nc.vector.scalar_tensor_tensor(out=tmp_f, in0=row_i, scalar=float(N), in1=tmp_f,
                                                op0=ALU.is_ge, op1=ALU.add))
            link(nc.vector.scalar_tensor_tensor(out=row_f, in0=tmp_f, scalar=FAR, in1=row_i,
                                                op0=ALU.mult, op1=ALU.add))
            first, span = sched_f[:, :, 1], sched_f[:, :, 0]
            link(nc.vector.tensor_reduce(first, row_f, AX_X, ALU.min))
            link(nc.vector.tensor_scalar(first, first, float(N), None, ALU.min))
            for h in range(2):
                nc.vector.tensor_scalar(row_f[:, h, :], row_f[:, h, :], sched_f[:, h, 1:2], None,
                                        ALU.subtract).then_inc(s_rel, 1)
            dve.wait_ge(s_rel, 2)
            link(nc.vector.scalar_tensor_tensor(out=tmp_f, in0=tmp_f, scalar=-2 * FAR, in1=row_f,
                                                op0=ALU.mult, op1=ALU.add))
            link(nc.vector.tensor_reduce(span, tmp_f, AX_X, ALU.max))
            link(nc.vector.tensor_scalar(sched_i[:, :], span, 0.0, None, ALU.max))
            link(nc.vector.tensor_scalar(sched_i[:, :], sched_i[:, :], P.bit_length() - 1, None,
                                         ALU.arith_shift_right))
            nc.vector.tensor_scalar(span, sched_i[:, :], 1.0, None, ALU.add).then_inc(s_rel, 1)
            dve.wait_ge(s_sess_in, 48)
            link(nc.vector.tensor_scalar(mask[:, :], inputs_i, 0.0, None, ALU.not_equal))
            link(nc.vector.tensor_reduce(rcnt3[:, :], mask[:, :].rearrange("p (t l) -> p t l", t=T), AX_X,
                                         ALU.add))
            link(nc.vector.tensor_scalar(rcnt3[:, :], rcnt3[:, :], 3.0, None, ALU.mult))
            nc.vector.reciprocal(rcnt3[:, :], rcnt3[:, :]).then_inc(s_mask, 1)

            dve.wait_ge(s_sched, 1)
            dve.wait_ge(s_const, 3)
            dve.wait_ge(s_zero, 1)
            rounds = dve.alloc_register("dve_rounds")
            steps = dve.alloc_register("dve_steps")
            window = dve.alloc_register("dve_window")
            n_rounds = dve.alloc_register("dve_n_rounds")
            one = dve.alloc_register("dve_one")
            dve.reg_mov(one, 1)
            dve.reg_mov(rounds, 0)
            dve.reg_mov(steps, 0)

            def place(slot, tiles):
                for j in range(tiles):
                    last = nc.vector.tensor_scalar(onehot[:, j, :], iota[:, :], edge_slot[:, slot, j:j + 1],
                                                   edge_slot[:, slot, TG + j:TG + j + 1],
                                                   ALU.is_equal, ALU.mult)
                last.then_inc(s_onehot, 1)

            def add_window():
                dve.reg_add(rounds, rounds, 1)
                at = dve.snap(window, min_val=0, max_val=N)
                dve.wait_ge(s_window, rounds)
                return nc.vector.tensor_tensor(sumT[:, bass.ds(at, P)], sumT[:, bass.ds(at, P)],
                                               bank[0][:, 0:P], ALU.add)

            def layer_group(layer, beside=None):
                def add_group(g, i, slot, tiles):
                    dve.wait_ge(s_edge, g + (layer * NG + 1))
                    place(slot, tiles)
                    dve.reg_load(n_rounds, sched[0:1, bass.ds(g * 2, 1)])
                    dve.reg_load(window, sched[0:1, bass.ds(g * 2 + 1, 1)])
                    if beside is not None:
                        beside(g)
                    add_window()
                    with dve.If_lt(one, n_rounds):
                        with dve.Fori(1, n_rounds):
                            dve.reg_add(steps, steps, 1)
                            nc.vector.tensor_scalar(edge_slot[:, slot, 0:TG], edge_slot[:, slot, 0:TG],
                                                    float(P), None, ALU.subtract).then_inc(s_dec, 1)
                            dve.reg_add(window, window, P)
                            dve.reg_alu(window, window, N, ALU.min)
                            dve.wait_ge(s_dec, steps)
                            place(slot, tiles)
                            add_window()
                    nc.vector.memset(small[:, 7:8], 0.0).then_inc(s_group, 1)
                return add_group

            def item_indices(n, at, t_at):
                lane, neg = idx_l[:, 0, :], idx_l[:, 1, :]
                nc.vector.tensor_tensor(
                    pick, alias_i[:, bass.ds(at, IDX_L)].unsqueeze(2).broadcast_to([P, IDX_L, L]),
                    iota[:, 0:L].unsqueeze(1).broadcast_to([P, IDX_L, L]), ALU.is_equal).then_inc(s_pick, 1)
                dve.wait_ge(s_pick, n * 5 + 1)
                nc.vector.tensor_tensor(
                    pick, pick, items_i[:, bass.ds(t_at, L)].unsqueeze(1).broadcast_to([P, IDX_L, L]),
                    ALU.mult).then_inc(s_pick, 1)
                dve.wait_ge(s_pick, n * 5 + 2)
                nc.vector.tensor_reduce(lane, pick, AX_X, ALU.add).then_inc(s_pick, 1)
                dve.wait_ge(s_pick, n * 5 + 3)
                nc.vector.tensor_scalar(neg, lane, 0.0, float(N), ALU.is_lt, ALU.mult).then_inc(s_pick, 1)
                dve.wait_ge(s_pick, n * 5 + 4)
                nc.vector.tensor_tensor(lane, lane, neg, ALU.add).then_inc(s_pick, 1)
                dve.wait_ge(s_pick, n * 5 + 5)
                nc.vector.tensor_scalar(item_idx[:, bass.ds(at, IDX_L)], lane, 0.0, float(N - 1),
                                        ALU.max, ALU.min)

            with dve.Fori(0, T) as t:
                with dve.Fori(0, IDX_C // 2) as c:
                    i = t * (IDX_C // 2) + c
                    for slot in range(2):
                        layer_group(0, lambda g: item_indices(g, g * IDX_L, t * L))(i * 2 + slot, i, slot, TG)
            with dve.Fori(T * IDX_C // 2, PAIRS) as i:
                for slot in range(2):
                    layer_group(0)(i * 2 + slot, i, slot, TG)
            layer_group(0)(NG - 2, PAIRS, 0, TG)
            layer_group(0)(NG - 1, PAIRS, 1, TAIL_T)

            def norms(layer):
                for q in range(1, NQ, 2):
                    if q >= 4:
                        dve.wait_ge(s_ssq, layer * NQ + q - 3)
                    x = sumT[:, 512 * q:512 * q + quad(q) * P]
                    nc.vector.tensor_tensor(squares[:, q % 4, 0:quad(q) * P], x, x, ALU.mult).then_inc(s_sqD, 1)
                dve.wait_ge(s_norm, layer + 1)
                link(nc.vector.tensor_scalar(rinv[:, :], rinv[:, :], EPS, None, ALU.max))
                ins = nc.vector.reciprocal(rinv[:, :], rinv[:, :])
                ins.then_inc(s_rinv, 1)
                dve.wait_ge(s_rinv, layer + 1)

            norms(0)
            for q in range(NQ):
                if q % 4 == 3:
                    continue
                w = quad(q)
                dve.wait_ge(s_rowT, q + 1)
                nc.vector.tensor_tensor(h1_rows[:, 4 * q:4 * q + w, :],
                                        bank[q % 3][:, 0:w * P].rearrange("p (j d) -> p j d", j=w),
                                        rinv[:, 4 * q:4 * q + w].unsqueeze(2).broadcast_to([P, w, D]),
                                        ALU.mult).then_inc(s_rowsD, 1)

            dve.wait_ge(s_zero, NQ + 1)
            dve.wait_ge(s_base, 32)
            dve.wait_ge(s_rowsA, NQ // 4)

            def add_h1(i):
                at = i * D
                b = seq1[:, bass.ds(at, D)]
                nc.vector.tensor_tensor(b, b, seq0[:, bass.ds(at, D)], ALU.add)

            groups(dve, layer_group(1), add_h1)

            norms(1)
            for q in range(NQ):
                dve.wait_ge(s_rowT, NQ + q + 1)
                for j in range(quad(q)):
                    last = nc.vector.scalar_tensor_tensor(
                        out=base_rows[:, 4 * q + j, :], in0=bank[q % 3][:, j * P:(j + 1) * P],
                        scalar=rinv[:, 4 * q + j:4 * q + j + 1], in1=base_rows[:, 4 * q + j, :],
                        op0=ALU.mult, op1=ALU.add)
                last.then_inc(s_rowsD, 1)

            def step(s, par, half):
                own = seq[par]

                def norm_columns(q):
                    w = quad(q) * P
                    dve.wait_ge(s_nroot, q + 1)
                    r = squares[:, 2 + q % 2, 0:w]
                    x = sumT[:, 512 * q:512 * q + w]
                    link(nc.vector.tensor_scalar(r, r, (LAYERS + 1) * EPS, None, ALU.max))
                    link(nc.vector.reciprocal(r, r))
                    nc.vector.tensor_tensor(x, x, r, ALU.mult).then_inc(s_gn, 1)

                def weigh(c):
                    back, tp, ch = lagged(par, c, 2)
                    m = s * NC + (c - 2 - NC)
                    n = len(CH[ch])
                    l0 = CH[ch][0]
                    dve.wait_ge(s_beta, m + 1)
                    nc.vector.tensor_tensor(bm[:, ch % 2, 0:n], bank[4][:, tp * 64 + l0:tp * 64 + l0 + n],
                                            mask[:, bass.ds(s * L + (l0 - back * L), n)],
                                            ALU.mult).then_inc(s_bm, 1)
                    if not (isinstance(m, int) and m == 0):
                        dve.wait_ge(s_free, m)
                    dve.wait_ge(s_bm, m + 1)
                    for i, l in enumerate(CH[ch]):
                        acc, w = sess_acc[:, i, :], bm[:, ch % 2, i:i + 1]
                        if ch == 0:
                            last = nc.vector.tensor_scalar(acc, seq[tp][:, l, 0:D], w, None, ALU.mult)
                        else:
                            last = nc.vector.scalar_tensor_tensor(out=acc, in0=seq[tp][:, l, 0:D], scalar=w,
                                                                  in1=acc, op0=ALU.mult, op1=ALU.add)
                    last.then_inc(s_free, 1)

                for c in range(NC):
                    back, tp, ch = lagged(par, c, 1)
                    if have(s, back):
                        n = len(CH[ch])
                        m = s * NC + (c - 1 - NC)
                        slot = (par + c) % 2
                        dve.wait_ge(s_mm2, m + 1)
                        if ch == 0:
                            dve.wait_ge(s_qT, s)
                        if not (isinstance(m, int) and m < 2):
                            dve.wait_ge(s_beta, m - 1)
                        nc.vector.tensor_tensor(
                            two[:, slot, 0:n * P].rearrange("p (i b) -> p i b", i=n),
                            bank[2 + slot][:, 0:n * P].rearrange("p (i b) -> p i b", i=n),
                            qT[:, :].unsqueeze(1).broadcast_to([P, n, P]), ALU.add).then_inc(s_qadd, 1)
                    if c == 3 and have(s, 2):
                        row = selT[:, par, :]
                        dve.wait_ge(s_nn, s - 1)
                        nc.vector.tensor_scalar(small[:, 2:3], small[:, 1:2], (LAYERS + 1) * EPS, None,
                                                ALU.max).then_inc(s_sred, 1)
                        dve.wait_ge(s_sred, s * 3 - 4)
                        nc.vector.reciprocal(small[:, 3:4], small[:, 2:3]).then_inc(s_sred, 1)
                        dve.wait_ge(s_sred, s * 3 - 3)
                        nc.vector.tensor_scalar(row, row, small[:, 3:4], W_K, ALU.mult, ALU.mult).then_inc(s_sel, 1)
                    back, tp, uh, ks = score_slot(par, half, c)
                    if have(s, back) and len(ks) == 2:
                        k = ks[1]
                        j = k // BC
                        if k - 2 < BC * j:
                            n2 = (NB * tp + j) // 2
                            if not (isinstance(s, int) and uh * NB + n2 == 0):
                                dve.wait_ge(s_out[(tp + j) % 2], uh * (16 * NB) + 16 * n2)
                        dve.wait_ge(s_score, s * NS + (k + 1 - back * NS))
                        nc.vector.tensor_copy(stage[:, (tp + j) % 2, (k - BC * j) * SC:(k - BC * j + 1) * SC],
                                              bank[6][:, 0:SC]).then_inc(s_evD, 1)
                    if isinstance(s, int) and s * NC + c < NQ:
                        norm_columns(s * NC + c)
                    if have(s, 0):
                        full = 16 * len(CH[c])
                        dve.wait_ge(s_land[par][c], half * full + full)
                        if not (isinstance(s, int) and s == 0 and c == 0):
                            dve.wait_ge(s_hsum, s * NC + c)
                        for i, l in enumerate(CH[c]):
                            acc, mk = hs_acc[:, i, :], mask[:, bass.ds(s * L + l, 1)]
                            if c == 0:
                                last = nc.vector.tensor_scalar(acc, own[:, l, 0:D], mk, None, ALU.mult)
                            else:
                                last = nc.vector.scalar_tensor_tensor(out=acc, in0=own[:, l, 0:D], scalar=mk,
                                                                      in1=acc, op0=ALU.mult, op1=ALU.add)
                        last.then_inc(s_hsum, 1)
                    if c == NC - 1 and have(s, 0):
                        dve.wait_ge(s_hsum, s * NC + NC)
                        if have(s, 1):
                            dve.wait_ge(s_q, s)
                        nc.vector.tensor_reduce(hs_row[:, :], hs_acc[:, :, :].rearrange("p a d -> p d a"), AX_X,
                                                ALU.add).then_inc(s_hred, 1)
                        dve.wait_ge(s_hred, s + 1)
                        nc.vector.tensor_scalar(hs_row[:, :], hs_row[:, :], rcnt3[:, bass.ds(s, 1)], None,
                                                ALU.mult).then_inc(s_hs, 1)
                    if have(s, lagged(par, c, 2)[0]):
                        weigh(c)
                    if c == 1 and have(s, 2):
                        row = selT[:, par, :]
                        dve.wait_ge(s_free, s * NC - NC)
                        nc.vector.tensor_reduce(row, sess_acc[:, :, :].rearrange("p a d -> p d a"), AX_X,
                                                ALU.add).then_inc(s_sred, 1)
                        dve.wait_ge(s_sred, s * 3 - 5)
                        nc.vector.tensor_tensor_reduce(out=square_dump[:, :], in0=row, in1=row,
                                                       scale=1.0, scalar=0.0, op0=ALU.mult, op1=ALU.add,
                                                       accum_out=small[:, 0:1]).then_inc(s_n2, 1)

            session_steps(step, dve)

        @block.tensor
        def _(pe):
            pe.wait_ge(s_const, 3)
            n = 0
            for q, x, s, v in ((0, col_f, s_colf, 1), (1, row_f, s_rel, 2), (2, val_f, s_val, 48)):
                pe.wait_ge(s, v)
                for h in range(2):
                    for jj in range(2):
                        if n >= 4:
                            pe.wait_ge(s_tab, n - 3)
                        for j in range(4):
                            at = (4 * jj + j) * P
                            last = nc.tensor.transpose(bank[n % 4][:, j * HG:(j + 1) * HG],
                                                       x[:, h, at:at + P], ident[0:HG, 0:HG])
                        last.then_inc(s_tab_t, 1)
                        n += 1
            pe.wait_ge(s_rel, 3)
            for h in range(2):
                for k in range(2):
                    last = nc.tensor.transpose(bank[4][0:1, (2 * h + k) * HG:(2 * h + k + 1) * HG],
                                               sched_f[:, h, k:k + 1], ident[0:HG, 0:HG])
            last.then_inc(s_sched_t, 1)
            pe.wait_ge(s_w, 16 * 7)
            nc.tensor.transpose(bank[5][:, 0:L], pos_sb[0:L, :], ident[0:L, 0:L])
            nc.tensor.transpose(bank[6][:, 0:D], glu1_sb, ident[:, :])
            nc.tensor.transpose(bank[6][:, D:2 * D], glu2_sb, ident[:, :]).then_inc(s_w_t, 1)
            pe.wait_ge(s_w_c, 3)
            nc.tensor.matmul(bank[7][:, 0:L], w1a, hsT[:, 0:L], start=True, stop=True).then_inc(s_w_t, 1)

            pe.wait_ge(s_sched, 1)
            pe.wait_ge(s_tab, 12)
            pe.wait_ge(s_ones, 1)
            rounds = pe.alloc_register("pe_rounds")
            n_rounds = pe.alloc_register("pe_n_rounds")
            one = pe.alloc_register("pe_one")
            pe.reg_mov(one, 1)
            pe.reg_mov(rounds, 0)
            for layer in range(LAYERS):
                def sum_group(g, i, slot, tiles):
                    pe.reg_load(n_rounds, sched[0:1, bass.ds(g * 2, 1)])
                    pe.reg_add(rounds, rounds, 1)
                    pe.wait_ge(s_onehot, rounds)
                    for j in range(tiles):
                        pe.wait_ge(s_gath[slot][j], landed(layer, i, slot, j))
                        last = nc.tensor.matmul(bank[0][:, 0:P], gath[:, slot, j, :], onehot[:, j, :],
                                                start=(j == 0), stop=(j == tiles - 1))
                    last.then_inc(s_window, 1)
                    with pe.If_lt(one, n_rounds):
                        with pe.Fori(1, n_rounds):
                            pe.reg_add(rounds, rounds, 1)
                            pe.wait_ge(s_onehot, rounds)
                            for j in range(tiles):
                                last = nc.tensor.matmul(bank[0][:, 0:P], gath[:, slot, j, :], onehot[:, j, :],
                                                        start=(j == 0), stop=(j == tiles - 1))
                            last.then_inc(s_window, 1)

                groups(pe, sum_group)

                pe.wait_ge(s_group, (layer + 1) * NG + 2)

                def rows(q):
                    if q >= 3:
                        pe.wait_ge(*rows_by(layer, q - 3))
                    for j in range(quad(q)):
                        at = 512 * q + j * P
                        last = nc.tensor.transpose(bank[q % 3][:, j * P:(j + 1) * P], sumT[:, at:at + P], ident[:, :])
                    last.then_inc(s_rowT, 1)

                for q in range(NQ):
                    pe.wait_ge(*squared(layer, q))
                    for j in range(quad(q)):
                        last = nc.tensor.matmul(bank[7][:, 4 * q + j:4 * q + j + 1],
                                                squares[:, q % 4, j * P:(j + 1) * P], ones[:, 0:1],
                                                start=True, stop=True)
                    last.then_inc(s_ssq, 1)
                    if q < 3:
                        rows(q)
                for q in range(3, NQ + 4):
                    if q < NQ:
                        rows(q)
                    if layer == 1 and 3 <= q <= NQ + 2:
                        r = q - 3
                        pe.wait_ge(*rows_by(1, r))
                        if r >= 2:
                            pe.wait_ge(s_gtc, r - 1)
                        for j in range(quad(r)):
                            last = nc.tensor.transpose(bank[3 + r % 2][:, j * P:(j + 1) * P],
                                                       base_rows[:, 4 * r + j, :], ident[:, :])
                        last.then_inc(s_gt, 1)
                    if layer == 1 and q >= 4:
                        r = q - 4
                        pe.wait_ge(s_gtc, r + 1)
                        if r >= 2:
                            pe.wait_ge(s_g1c, r - 1)
                        for j in range(quad(r)):
                            at = 512 * r + j * P
                            last = nc.tensor.matmul(bank[5 + r % 2][:, j * D:(j + 1) * D], sumT[:, at:at + P],
                                                    w1b, start=True, stop=True)
                        last.then_inc(s_g1, 1)

            def step(s, par, half):
                def score(c, which):
                    back, tp, uh, ks = score_slot(par, half, c)
                    if not have(s, back) or which >= len(ks):
                        return
                    k = ks[which]
                    if k == 0:
                        pe.wait_ge(s_selT, s - 1)
                    if not (isinstance(s, int) and s - back == 0 and k < 2):
                        if k % 2 == 0:
                            pe.wait_ge(s_evA, s * NS_A + (k // 2 - back * NS_A))
                        else:
                            pe.wait_ge(s_evD, s * NS_D + (k // 2 - back * NS_D))
                    nc.tensor.matmul(bank[5 + k % 2][:, 0:SC], selT[:, tp, :], sumT[:, k * SC:(k + 1) * SC],
                                     start=True, stop=True).then_inc(s_score, 1)

                if isinstance(s, int) and s == 2:
                    pe.wait_ge(s_gn, NQ)
                for c in range(NC):
                    if have(s, 1):
                        slot = (par + 1 + c) % 2
                        w = len(CH[c]) * P
                        m = s * NC + (c - NC)
                        pe.wait_ge(s_tanh, m + 1)
                        if not (isinstance(m, int) and m < 2):
                            pe.wait_ge(s_qadd, m - 1)
                        nc.tensor.matmul(bank[2 + slot][:, 0:w], glu1T[:, :], nh[:, c, 0:w],
                                         start=True, stop=True).then_inc(s_mm2, 1)
                    if isinstance(s, int) and s * NC + c < NQ:
                        q = s * NC + c
                        w = quad(q) * P
                        pe.wait_ge(s_nsq, q + 1)
                        if q >= 2:
                            pe.wait_ge(s_nroot, q - 1)
                        nc.tensor.matmul(bank[5 + q % 2][:, 0:w], ones, squares[:, q % 2, 0:w],
                                         start=True, stop=True).then_inc(s_nsum, 1)
                    if c == 0 and have(s, 1):
                        pe.wait_ge(s_hs, s)
                        nc.tensor.transpose(bank[7][:, 0:P], hs_row[:, :], ident[:, :]).then_inc(s_hst, 1)
                    score(c, 0)
                    if c == 0 and have(s, 1):
                        pe.wait_ge(s_hsT, s)
                        nc.tensor.matmul(bank[7][:, P:2 * P], glu2T[:, :], hsT[:, :], start=True,
                                         stop=True).then_inc(s_q, 1)
                    if c == 3 and have(s, 2):
                        pe.wait_ge(s_sel, s - 1)
                        if have(s, 1):
                            pe.wait_ge(s_qT, s)
                        nc.tensor.transpose(bank[7][:, 2 * P:3 * P], selT[:, par, :], ident[:, :]).then_inc(s_selt, 1)
                    score(c, 1)
                    back, tp, ch = lagged(par, c, 2)
                    if have(s, back):
                        m = s * NC + (c - 2 - NC)
                        slot = (par + 1 + c) % 2
                        pe.wait_ge(s_sig, m + 1)
                        if not (isinstance(m, int) and m == 0):
                            pe.wait_ge(s_bm, m)
                        for i, l in enumerate(CH[ch]):
                            last = nc.tensor.matmul(bank[4][:, tp * 64 + l:tp * 64 + l + 1],
                                                    two[:, slot, i * P:(i + 1) * P], w2c[:, :],
                                                    start=True, stop=True)
                        last.then_inc(s_beta, 1)
                    if have(s, 0):
                        full = 16 * len(CH[c])
                        pe.wait_ge(s_land[par][c], half * full + full)
                        if not (isinstance(s, int) and s == 0 and c < 2):
                            pe.wait_ge(s_tanh, s * NC + (c - 1))
                        for i, l in enumerate(CH[c]):
                            last = nc.tensor.transpose(bank[(par + c) % 2][:, i * P:(i + 1) * P],
                                                       seq[par][:, l, D:2 * D], ident[:, :])
                        last.then_inc(s_g1t, 1)

            session_steps(step, pe)


_INS = ['r_items', 'r_inputs', 'r_alias_inputs', 'L0_rec_adj_row', 'L0_rec_adj_col', 'L0_rec_adj_val', 'L0_rec_E',
        'L0_rec_pos_emb', 'L0_rec_w1', 'L0_rec_w2', 'L0_rec_glu1_w', 'L0_rec_glu1_b', 'L0_rec_glu2_w']


def kernel(**inputs):
    import numpy as _np
    import concourse.bacc as _bacc
    from concourse import mybir as _mybir
    from concourse.bass_utils import run_bass_kernel_spmd as _run

    nc = _bacc.Bacc("TRN2", target_bir_lowering=False, num_devices=1)
    arrays, args = {}, []
    for name in _INS:
        a = _np.ascontiguousarray(inputs[name])
        arrays[f"in_{name}_dram"] = a
        args.append(nc.dram_tensor(f"in_{name}_dram", a.shape, _mybir.dt.from_np(a.dtype), kind="ExternalInput").ap())
    shape = (inputs['r_items'].shape[0], inputs['L0_rec_E'].shape[0])
    args.append(nc.dram_tensor("out_0_dram", shape, _mybir.dt.float32, kind="ExternalOutput").ap())
    build(nc, *args)
    r = _run(nc, [arrays], core_ids=[0])
    return r.results[0]["out_0_dram"]
```

```python
from contextlib import ExitStack

import concourse.bass as bass
from concourse import mybir

F32 = mybir.dt.float32
I32 = mybir.dt.int32
U32 = mybir.dt.uint32
ALU = mybir.AluOpType
ACT = mybir.ActivationFunctionType
AX_X = mybir.AxisListType.X

P = 128
EPS = 1e-12
W_K = 12.0
LAYERS = 2
FAR = 1e10


def build(nc, items, inputs, alias, adj_row, adj_col, adj_val, E, pos_emb, w1, w2,
          glu1_w, glu1_b, glu2_w, out):
    N, D = E.shape
    S, L = items.shape
    NNZ = adj_row.shape[0]
    assert D == P and S % P == 0 and L <= P

    TG = 8
    EG = TG * P
    NG = -(-NNZ // EG)
    HG = NG // 2
    TAIL = NNZ - (NG - 1) * EG
    TAIL_T = -(-TAIL // P)
    assert NG == 2 * HG and HG <= P

    NT = -(-N // P)
    NQ = -(-NT // 4)
    NP_ = NT * P
    LAST_T = N - (NT - 1) * P
    assert NT <= L * 2
    MG = 4 * P * NNZ // N // EG
    NM = NG // MG
    LATE = 2
    assert 4 * P == 1 << ((4 * P).bit_length() - 1) and 4 * P % MG == 0
    assert MG == TG == 8 and NM == NQ - 1 and NG - NM * MG == 4
    Q0, Q1 = NM - 1, NM

    def quad(q):
        return min(4, NT - 4 * q)

    T = S // P
    CH = [list(range(4 * c, min(4 * c + 4, L))) for c in range(-(-L // 4))]
    NC = len(CH)
    assert T % 2 == 0 and NC % 2 == 1
    IDX_L = 5
    IDX_C = L // IDX_L
    IDX_U = T // MG
    assert T % MG == 0 and IDX_C * IDX_U < NM

    SC = 500
    NS = N // SC
    BC = 3
    NB = -(-NS // BC)
    assert N <= L * 2 * D and NS * SC == N and NS % 2 == 1 and NB % 2 == 1
    SCORE_AT = 4

    h1_dram = nc.dram_tensor("h1_rows", (NP_, D), F32).ap()
    graph_dram = nc.dram_tensor("graph_rows", (NP_, 2 * D), F32).ap()

    with ExitStack() as ctx:
        def sb(name, shape, dt=F32):
            return ctx.enter_context(nc.sbuf_tensor(name, shape, dt))

        def sem(name):
            return ctx.enter_context(nc.semaphore(name))

        sumT = sb("sumT", [P, N + P])
        seq0 = sb("seq0", [P, L * 2 * D])
        seq1 = sb("seq1", [P, L * 2 * D])
        seq = [x[:, :].rearrange("p (l d) -> p l d", l=L) for x in (seq0, seq1)]
        h1_rows = seq0[:, 0:NT * D].rearrange("p (t d) -> p t d", d=D)
        base_rows = seq1[:, 0:NT * D].rearrange("p (t d) -> p t d", d=D)

        def raw(n, dt=F32):
            v = seq0[0:HG, 2 * EG * n:2 * EG * (n + 1)]
            return (v if dt is F32 else v.bitcast(dt)).rearrange("g (h n) -> g h n", h=2)

        row_i, col_i, val_f = raw(0, I32), raw(1, I32), raw(2)
        row_f, tmp_f, col_f = raw(3), raw(4), raw(5)

        work = sb("work", [P, 3 * TG * NG + 2 * TG * D])
        table = work[:, 0:3 * TG * NG].rearrange("p (q g) -> p q g", g=NG)
        gath = work[:, 3 * TG * NG:].rearrange("p (s j d) -> p s j d", s=2, j=TG)
        nh = work[:, 0:NC * 4 * P].rearrange("p (c n) -> p c n", c=NC)

        onehot_b = sb("onehot", [P, TG * P])
        onehot = onehot_b[:, :].rearrange("p (j r) -> p j r", j=TG)
        two = onehot_b[:, :].rearrange("p (s n) -> p s n", s=2)

        stage_b = sb("stage", [P, 2 * BC * SC])
        stage = stage_b[:, :].rearrange("p (s n) -> p s n", s=2)
        last_scores = seq0[:, 0:N]
        items_i = stage_b[:, 0:T * L].bitcast(I32)
        alias_i = stage_b[:, T * L:2 * T * L].bitcast(I32)
        inputs_i = stage_b[:, 2 * T * L:3 * T * L].bitcast(I32)
        pick = stage_b[:, 3 * T * L:3 * T * L + IDX_L * L].rearrange("p (l m) -> p l m", l=IDX_L)
        gn_rows = stage_b[:, 0:4 * D].rearrange("p (j d) -> p j d", j=4)
        gn_T = stage_b[:, 4 * D:8 * D]
        g1_out = stage_b[:, 8 * D:12 * D].rearrange("p (j d) -> p j d", j=4)

        item_idx = sb("item_idx", [P, (T + 1) * L], U32)
        mask = sb("mask", [P, T * L])
        ident = sb("ident", [P, P])
        glu1T = sb("glu1T", [P, D])
        glu2T = sb("glu2T", [P, D])
        posT = sb("posT", [P, L])
        w2c = sb("w2c", [P, 1])
        b1c = sb("b1c", [P, 1])
        hs_acc = sb("hs_acc", [P, 4, D])
        sess_acc = sb("sess_acc", [P, 4, D])
        hsT = sb("hsT", [P, P])
        qT = sb("qT", [P, P])
        sessT = sb("sessT", [P, 2, P])
        rcnt3 = sb("rcnt3", [P, T])
        bm = sb("bm", [P, 2, 4])
        small = sb("small", [P, 8])
        square_dump = sb("square_dump", [P, D])
        h_sq, h_norm, h_inv, g_sq, g_norm, g_inv, g_scale = (sb("row_" + x, [P, 4]) for x in (
            "h_sq", "h_norm", "h_inv", "g_sq", "g_norm", "g_inv", "g_scale"))
        idx_l = sb("idx_l", [P, 2, IDX_L])
        idx_slot = sb("idx_slot", [P, 2, TG], U32)
        edge_slot = sb("edge_slot", [P, 2, 2 * TG])
        sess_idx = sb("sess_idx", [P, 2, L], U32)
        sched_f = sb("sched_f", [HG, 2, 2])
        sched_i = sb("sched_i", [HG, 2], I32)
        iota = qT
        w1b = sessT[:, 0, :]
        sched = hs_acc[0:1, :, :].rearrange("o a b -> o (a b)")[:, 0:2 * NG].bitcast(I32)
        sorted_i = hs_acc[0:1, :, :].rearrange("o a b -> o (a b)")[:, 2 * NG:2 * NG + 1].bitcast(I32)
        bound, in_order = onehot_b[0:1, 0:NG].bitcast(I32), onehot_b[0:1, 2 * P:2 * P + NG - LATE]
        pos_sb, glu1_sb, glu2_sb, w1a = (sess_acc[:, i, :] for i in range(4))
        quadT = sess_acc[:, :, :].rearrange("p a d -> p (a d)")
        hs_row = hsT

        bank = [ctx.enter_context(nc.psum_tensor(f"bank{b}", [P, 512], F32)) for b in range(8)]

        s_pad = sem("s_pad")
        s_row, s_col, s_val = sem("s_row"), sem("s_col"), sem("s_val")
        s_w = sem("s_w")
        s_sess_in = sem("s_sess_in")
        s_base = sem("s_base")
        s_const = sem("s_const")
        s_colf = sem("s_colf")
        s_rel = sem("s_rel")
        s_tab_t = sem("s_tab_t")
        s_tab = sem("s_tab")
        s_sched_t, s_sched = sem("s_sched_t"), sem("s_sched")
        s_w_t, s_w_c = sem("s_w_t"), sem("s_w_c")
        s_mask = sem("s_mask")
        s_gidx = sem("s_gidx")
        s_edge = sem("s_edge")
        s_gath = [[sem(f"s_gath{i}_{j}") for j in range(TG)] for i in range(2)]
        s_onehot = sem("s_onehot")
        s_window = sem("s_window")
        s_group = sem("s_group")
        s_sorted = sem("s_sorted")
        s_quadT = sem("s_quadT")
        s_zero = sem("s_zero")
        s_rowT = sem("s_rowT")
        s_ssq, s_norm, s_inv = sem("s_ssq"), sem("s_norm"), sem("s_inv")
        s_rows = sem("s_rows")
        s_h1 = sem("s_h1")
        s_gsq, s_gnorm, s_ginv = sem("s_gsq"), sem("s_gnorm"), sem("s_ginv")
        s_gn = sem("s_gn")
        s_gt, s_gtc = sem("s_gt"), sem("s_gtc")
        s_gcol = sem("s_gcol")
        s_g1, s_g1c = sem("s_g1"), sem("s_g1c")
        s_gst = sem("s_gst")
        s_gr = sem("s_gr")
        s_sidx_pad = sem("s_sidx_pad")
        s_sidx = sem("s_sidx")
        s_land = [[sem(f"s_land{i}_{c}") for c in range(NC)] for i in range(2)]
        s_g1t = sem("s_g1t")
        s_tanh = sem("s_tanh")
        s_mm2, s_qadd, s_sig = sem("s_mm2"), sem("s_qadd"), sem("s_sig")
        s_beta = sem("s_beta")
        s_free = sem("s_free")
        s_link, s_dec, s_pick = sem("s_link"), sem("s_dec"), sem("s_pick")
        s_bm, s_hsum, s_hred, s_sred = (sem(x) for x in ("s_bm", "s_hsum", "s_hred", "s_sred"))
        s_hs, s_hst, s_hsT, s_q, s_qT = (sem(x) for x in ("s_hs", "s_hst", "s_hsT", "s_q", "s_qT"))
        s_n2, s_nn, s_scale = sem("s_n2"), sem("s_nn"), sem("s_scale")
        s_sess, s_sesst, s_sessT = sem("s_sess"), sem("s_sesst"), sem("s_sessT")
        s_score = sem("s_score")
        s_scored = sem("s_scored")
        s_pool, s_sp = sem("s_pool"), sem("s_sp")
        s_out = [sem("s_out0"), sem("s_out1")]
        s_last = sem("s_last")

        def edges(x, half):
            if half == 0:
                return x[0:HG * EG].rearrange("(g n) -> g n", n=EG)
            return x[HG * EG:(NG - 1) * EG].rearrange("(g n) -> g n", n=EG)

        def by_tile(x):
            return x.rearrange("(p t) l -> p (t l)", t=T)

        graph_v = graph_dram.rearrange("(t p) c -> p t c", p=P)
        h1_v = h1_dram.rearrange("(t p) c -> p t c", p=P)
        out_v = out.rearrange("(p t) n -> p t n", t=T)

        def landed(layer, i, slot, j):
            per_layer = HG - (slot == 1 and j >= TAIL_T)
            return i * 16 + 16 * (1 + layer * per_layer)

        def macro(m, bodies, beside):
            for k in range(MG):
                bodies[k](m * MG + k, m * (MG // 2) + k // 2, k % 2, TG)
                beside(k)

        def layer_steps(eng, layer, body, ordered, one, finish, after, closing, index=None, masks=None,
                        last_body=None, start=0):
            def finish_beside(q):
                def beside(k):
                    if k in after:
                        with eng.If_eq(ordered, one):
                            for part, at in enumerate(after):
                                if at == k:
                                    finish(q, part, q * MG + (layer * NG + MG + LATE))
                return beside

            def finish_whole(q, groups):
                for part in range(len(after)):
                    finish(q, part, layer * NG + groups)

            def closing_parts(k):
                if k in closing:
                    with eng.If_eq(ordered, one):
                        for q, part in closing[k]:
                            finish(q, part, layer * NG + (NM * MG + LATE if q < NM else NG))

            with eng.Fori(start, MG // 2) as i:
                body(i * 2, i, 0, TG)
                body(i * 2 + 1, i, 1, TG)
            first = 1
            if index is not None:
                masks()
                with eng.Fori(0, IDX_C) as c:
                    with eng.Fori(0, IDX_U) as u:
                        q = c * IDX_U + u
                        macro(q + 1, index(c, u), finish_beside(q))
                first += IDX_C * IDX_U
            with eng.Fori(first, NM) as m:
                macro(m, [body] * MG, finish_beside(m - 1))
            for g in range(NM * MG, NG - 1):
                body(g, g // 2, g % 2, TG)
                closing_parts(g - NM * MG)
            (last_body or body)(NG - 1, (NG - 1) // 2, 1, TAIL_T)
            closing_parts(NG - 1 - NM * MG)
            with eng.If_lt(ordered, one):
                with eng.Fori(0, NM) as q:
                    finish_whole(q, NG)
                finish_whole(NM, NG)

        def session_steps(step, eng):
            for s in range(4):
                step(s, s % 2, s // 2)
            with eng.Fori(2, T // 2) as v:
                step(v * 2, 0, v)
                step(v * 2 + 1, 1, v)
            for s in range(T, T + 3):
                step(s, s % 2, s // 2)

        def have(s, back):
            return not isinstance(s, int) or 0 <= s - back < T

        def lagged(par, c, lag):
            if c >= lag:
                return 1, 1 - par, c - lag
            return 2, par, c - lag + NC

        def score_slot(par, half, c):
            if c >= SCORE_AT:
                k = 2 * (c - SCORE_AT)
                return 2, par, half - 1, [k, k + 1]
            k = 2 * (c - SCORE_AT + NC)
            return 3, 1 - par, half - 2 + par, [x for x in (k, k + 1) if x < NS]

        block = ctx.enter_context(nc.Block())

        @block.sync
        def _(sp):
            for x, dst, s in ((adj_col, col_i, s_col), (adj_row, row_i, s_row), (adj_val, val_f, s_val)):
                sp.dma_start(dst[:, 0, :], edges(x, 0)).then_inc(s, 16)
                if x is adj_col:
                    sp.wait_ge(s_pad, 3)
                sp.dma_start(dst[0:HG - 1, 1, :], edges(x, 1)).then_inc(s, 16)
                sp.dma_start(dst[HG - 1:HG, 1, 0:TAIL],
                             x[(NG - 1) * EG:NNZ].rearrange("(g n) -> g n", g=1)).then_inc(s, 16)
            for dst, src in ((w1a, w1[0:D, :]), (w1b, w1[D:2 * D, :]), (pos_sb[0:L, :], pos_emb),
                             (glu1_sb, glu1_w), (glu2_sb, glu2_w), (w2c[:, :], w2),
                             (b1c[:, :], glu1_b.rearrange("(p o) -> p o", o=1))):
                sp.dma_start(dst, src).then_inc(s_w, 16)
            sp.wait_ge(s_group, 4)
            for dst, src in ((items_i, items), (alias_i, alias), (inputs_i, inputs)):
                sp.dma_start(dst, by_tile(src)).then_inc(s_sess_in, 16)
            sp.wait_ge(s_pad, 4)
            for q in range(NQ):
                if q < NQ - 1:
                    sp.dma_start(base_rows[:, 4 * q:4 * q + 4, :],
                                 E[512 * q:512 * q + 512, :].rearrange("(t p) d -> p t d", p=P)).then_inc(s_base, 16)
                else:
                    for t in range(4 * q, NT - 1):
                        sp.dma_start(base_rows[:, t, :], E[t * P:t * P + P, :]).then_inc(s_base, 16)
                    sp.dma_start(base_rows[0:LAST_T, NT - 1, :], E[(NT - 1) * P:N, :]).then_inc(s_base, 16)
                sp.wait_ge(s_rows, q + 1)
                sp.dma_start(h1_v[:, 4 * q:4 * q + quad(q), :],
                             h1_rows[:, 4 * q:4 * q + quad(q), :]).then_inc(s_h1, 16)
            for q in range(NQ):
                t0, t1 = 4 * q, 4 * q + quad(q)
                sp.wait_ge(s_rows, NQ + q + 1)
                sp.dma_start(graph_v[:, t0:t1, 0:D], base_rows[:, t0:t1, :]).then_inc(s_gr, 16)
                sp.wait_ge(s_g1c, q + 1)
                sp.dma_start(graph_v[:, t0:t1, D:2 * D], g1_out[:, 0:quad(q), :]).then_inc(s_gst, 16)

            def store_tile(u, par):
                for j in range(NB):
                    end = min(BC * (j + 1), NS)
                    sp.wait_ge(s_scored, u * NS + end)
                    sp.sem_inc(s_sp, 1)
                    slot = (par + j) % 2
                    sp.dma_start(out_v[:, bass.ds(u, 1), BC * SC * j:SC * end],
                                 stage[:, slot:slot + 1, 0:SC * end - BC * SC * j]).then_inc(s_out[slot], 16)

            with sp.Fori(0, T // 2 - 1) as v:
                store_tile(v * 2, 0)
                store_tile(v * 2 + 1, 1)
            store_tile(T - 2, 0)
            for j in range(NB):
                end = min(BC * (j + 1), NS)
                sp.wait_ge(s_scored, (T - 1) * NS + end)
                sp.dma_start(out_v[:, T - 1:T, BC * SC * j:SC * end],
                             last_scores[:, BC * SC * j:SC * end].unsqueeze(1)).then_inc(s_last, 16)
            sp.wait_ge(s_out[0], 16 * ((T - 1) * NB - (T - 1) * NB // 2))
            sp.wait_ge(s_out[1], 16 * ((T - 1) * NB // 2))
            sp.wait_ge(s_last, 16 * NB)

        @block.gpsimd
        def _(pool):
            nc.gpsimd.iota(iota[:, :], [[1, P]], base=0, channel_multiplier=0,
                           allow_small_or_imprecise_dtypes=True).then_inc(s_const, 1)
            nc.gpsimd.iota(ident[:, :], [[1, P]], base=0, channel_multiplier=-1,
                           allow_small_or_imprecise_dtypes=True).then_inc(s_const, 1)
            pool.wait_ge(s_const, 2)
            nc.gpsimd.tensor_scalar(ident[:, :], ident[:, :], 0.0, None, ALU.is_equal).then_inc(s_const, 1)
            pool.wait_ge(s_const, 3)
            nc.gpsimd.iota(onehot_b[:, 0:NG].bitcast(I32), [[4 * P // MG, NG]], base=0, channel_multiplier=0,
                           allow_small_or_imprecise_dtypes=True).then_inc(s_const, 1)
            nc.gpsimd.memset(item_idx[:, T * L:(T + 1) * L], 0).then_inc(s_sidx_pad, 1)
            nc.gpsimd.memset(sumT[:, :], 0.0).then_inc(s_zero, 1)

            for layer in range(LAYERS):
                src = E if layer == 0 else h1_dram
                if layer == 1:
                    pool.wait_ge(s_h1, 16 * NQ)

                def gather(g, i, slot, tiles):
                    pool.wait_ge(s_gidx, g + (layer * NG + 1))
                    pool.sem_inc(s_pool, 1)
                    for j in range(tiles):
                        nc.gpsimd.indirect_dma_start(
                            out=gath[:, slot, j, :], out_offset=None, in_=src,
                            in_offset=bass.IndirectOffsetOnAxis(ap=idx_slot[:, slot, j:j + 1], axis=0),
                        ).then_inc(s_gath[slot][j], 16)

                with pool.Fori(0, NG // 2 - 1) as i:
                    gather(i * 2, i, 0, TG)
                    gather(i * 2 + 1, i, 1, TG)
                gather(NG - 2, NG // 2 - 1, 0, TG)
                gather(NG - 1, NG // 2 - 1, 1, TAIL_T)

            pool.wait_ge(s_gr, 16 * NQ)
            pool.wait_ge(s_gst, 16 * (NQ + 1))

            def step(s, par, half):
                if not have(s, 0):
                    return
                pool.wait_ge(s_sidx, s + 1)
                pool.sem_inc(s_pool, 1)
                for c in range(NC):
                    if have(s, 2):
                        pool.wait_ge(s_free, s * NC + (c + 1 - 2 * NC))
                        pool.sem_inc(s_pool, 1)
                    for l in CH[c]:
                        nc.gpsimd.indirect_dma_start(
                            out=seq[par][:, l, :], out_offset=None, in_=graph_dram,
                            in_offset=bass.IndirectOffsetOnAxis(ap=sess_idx[:, par, l:l + 1], axis=0),
                        ).then_inc(s_land[par][c], 16)

            session_steps(step, pool)

        @block.scalar
        def _(act):
            def copy_table(n):
                q, h, jj = n // 4, n // 2 % 2, n % 2
                act.wait_ge(s_tab_t, n + 1)
                nc.scalar.copy(table[:, q * TG + 4 * jj:q * TG + 4 * jj + 4, h * HG:(h + 1) * HG],
                               bank[n % 4][:, 0:4 * HG].rearrange("p (j g) -> p j g", j=4)).then_inc(s_tab, 1)

            def stage_indices(g, slot):
                nc.scalar.copy(idx_slot[:, slot, :], table[:, 0:TG, bass.ds(g, 1)]
                               .rearrange("p q o -> p (q o)")).then_inc(s_gidx, 1)

            def stage_edges(g, slot):
                nc.scalar.copy(edge_slot[:, slot, :], table[:, TG:3 * TG, bass.ds(g, 1)]
                               .rearrange("p q o -> p (q o)")).then_inc(s_edge, 1)

            for n in range(4):
                copy_table(n)
            act.wait_ge(s_tab, 4)
            for g in range(2):
                stage_indices(g, g)
            for n in range(4, 12):
                copy_table(n)
            act.wait_ge(s_tab, 12)
            for g in range(2):
                stage_edges(g, g)
            act.wait_ge(s_sched_t, 1)
            nc.scalar.copy(sched.rearrange("o (h g k) -> o h k g", h=2, k=2),
                           bank[4][0:1, 0:4 * HG].rearrange("o (h k g) -> o h k g", h=2, k=2)).then_inc(s_sched, 1)
            act.wait_ge(s_w_t, 1)
            nc.scalar.copy(hsT[:, 0:L], bank[5][:, 0:L]).then_inc(s_w_c, 1)
            nc.scalar.copy(glu1T[:, :], bank[6][:, 0:D]).then_inc(s_w_c, 1)
            nc.scalar.copy(glu2T[:, :], bank[6][:, D:2 * D]).then_inc(s_w_c, 1)
            act.wait_ge(s_w_t, 2)
            nc.scalar.copy(posT[:, :], bank[7][:, 0:L]).then_inc(s_w_c, 1)

            act.wait_ge(s_sorted, 1)
            one, ordered = act.alloc_register("act_one"), act.alloc_register("act_ordered")
            act.reg_mov(one, 1)
            act.reg_load(ordered, sorted_i)
            for layer in range(LAYERS):
                def stage_group(g, i, slot, tiles):
                    act.wait_ge(s_group, g + (layer * NG + 1))
                    stage_indices(g, slot)
                    stage_edges(g, slot)

                def finish(q, part, base):
                    n = q + layer * NQ
                    w = quad(q) if isinstance(q, int) else 4
                    if part == 0:
                        act.wait_ge(s_rowT, n + 1)
                        for j in range(w):
                            last = nc.scalar.activation(bank[4][:, j * D:(j + 1) * D], bank[1][:, j * D:(j + 1) * D],
                                                        ACT.Square, accum_out=h_sq[:, j:j + 1])
                        last.then_inc(s_ssq, 1)
                        act.wait_ge(s_ssq, n + 1)
                        nc.scalar.activation(h_norm[:, 0:w], h_sq[:, 0:w], ACT.Sqrt).then_inc(s_norm, 1)
                    elif part == 1:
                        act.wait_ge(s_rows, n + 1)
                        for j in range(w):
                            last = nc.scalar.activation(bank[4][:, j * D:(j + 1) * D],
                                                        seq1[:, bass.ds(q * (4 * D) + j * D, D)],
                                                        ACT.Square, accum_out=g_sq[:, j:j + 1])
                        last.then_inc(s_gsq, 1)
                        act.wait_ge(s_gsq, q + 1)
                        nc.scalar.activation(g_norm[:, 0:w], g_sq[:, 0:w], ACT.Sqrt).then_inc(s_gnorm, 1)
                    else:
                        act.wait_ge(s_gt, q + 1)
                        nc.scalar.copy(gn_T[:, 0:w * P], bank[2][:, 0:w * P]).then_inc(s_gtc, 1)

                layer_steps(act, layer, stage_group, ordered, one, finish, (4,) if layer == 0 else (4, 5, 7),
                            {3: [(Q0, 0), (Q1, 0)] if layer == 0 else
                                [(Q0, 0), (Q0, 1), (Q1, 0), (Q0, 2), (Q1, 1), (Q1, 2)]}, start=1 - layer)

            act.wait_ge(s_sidx_pad, 1)
            nc.scalar.copy(sess_idx[:, 0, :], item_idx[:, 0:L]).then_inc(s_sidx, 1)

            def step(s, par, half):
                if have(s, 0):
                    nc.scalar.copy(sess_idx[:, 1 - par, :],
                                   item_idx[:, bass.ds(s * L + L, L)]).then_inc(s_sidx, 1)
                for c in range(NC):
                    if c == 1 and have(s, 1):
                        act.wait_ge(s_q, s)
                        nc.scalar.activation(qT[:, :], bank[7][:, P:2 * P], ACT.Identity,
                                             bias=b1c[:, 0:1]).then_inc(s_qT, 1)
                    back, tp, ch = lagged(par, c, 1)
                    if have(s, back):
                        w = len(CH[ch]) * P
                        b = (par + c) % 2
                        act.wait_ge(s_qadd, s * NC + (c - NC))
                        nc.scalar.activation(two[:, b, 0:w], two[:, b, 0:w], ACT.Sigmoid).then_inc(s_sig, 1)
                    back, tp, uh, ks = score_slot(par, half, c)
                    if have(s, back):
                        for k in ks:
                            j = k // BC
                            if k == 0:
                                act.wait_ge(s_scale, s - 1)
                            last = isinstance(s, int) and s - back == T - 1
                            if k == BC * j and not last:
                                n2 = (NB * tp + j) // 2
                                if not (isinstance(s, int) and uh * NB + n2 == 0):
                                    act.wait_ge(s_out[(tp + j) % 2], uh * (16 * NB) + 16 * n2)
                            act.wait_ge(s_score, s * NS + (k + 1 - back * NS))
                            nc.scalar.activation(
                                last_scores[:, k * SC:(k + 1) * SC] if last else
                                stage[:, (tp + j) % 2, (k - BC * j) * SC:(k - BC * j + 1) * SC],
                                bank[5 + k % 2][:, 0:SC], ACT.Copy,
                                scale=small[:, 4 + tp:5 + tp]).then_inc(s_scored, 1)
                    if c == 0 and have(s, 1):
                        act.wait_ge(s_hst, s)
                        nc.scalar.copy(hsT[:, :], bank[7][:, 0:P]).then_inc(s_hsT, 1)
                    if c == 2 and have(s, 2):
                        act.wait_ge(s_n2, s - 1)
                        nc.scalar.activation(small[:, 1:2], small[:, 0:1], ACT.Sqrt).then_inc(s_nn, 1)
                    if c == 3 and have(s, 2):
                        act.wait_ge(s_sesst, s - 1)
                        nc.scalar.copy(sessT[:, par, :], bank[7][:, 2 * P:3 * P]).then_inc(s_sessT, 1)
                    if have(s, 0):
                        act.wait_ge(s_g1t, s * NC + (c + 1))
                        if have(s, 1):
                            act.wait_ge(s_mm2, s * NC + (c + 1 - NC))
                        for i, l in enumerate(CH[c]):
                            last = nc.scalar.activation(nh[:, c, i * P:(i + 1) * P],
                                                        bank[(par + c) % 2][:, i * P:(i + 1) * P], ACT.Tanh,
                                                        bias=posT[:, L - 1 - l:L - l])
                        last.then_inc(s_tanh, 1)

            session_steps(step, act)

        @block.vector
        def _(dve):
            last = slice((HG - 1) // 32 * 32, HG)
            nc.vector.memset(row_i[last, 1, :], N).then_inc(s_pad, 1)
            nc.vector.memset(col_i[last, 1, :], 0).then_inc(s_pad, 1)
            nc.vector.memset(val_f[last, 1, :], 0.0).then_inc(s_pad, 1)
            nc.vector.memset(base_rows[:, NT - 1, :], 0.0).then_inc(s_pad, 1)
            chain = [0]

            def link(ins):
                chain[0] += 1
                ins.then_inc(s_link, 1)
                dve.wait_ge(s_link, chain[0])

            nc.vector.memset(small[:, 7:8], 0.0).then_inc(s_group, 2)
            nc.vector.memset(small[:, 6:7], 0.0).then_inc(s_gst, 16)
            dve.wait_ge(s_col, 48)
            link(nc.vector.tensor_scalar(tmp_f, col_i, 0.0, float(N), ALU.is_lt, ALU.mult))
            link(nc.vector.tensor_tensor(col_f, tmp_f, col_i, ALU.add))
            nc.vector.tensor_scalar(col_f, col_f, 0.0, float(N - 1), ALU.max, ALU.min).then_inc(s_colf, 1)
            dve.wait_ge(s_row, 48)
            link(nc.vector.tensor_scalar(tmp_f, row_i, 0.0, None, ALU.is_lt))
            link(nc.vector.scalar_tensor_tensor(out=tmp_f, in0=row_i, scalar=float(N), in1=tmp_f,
                                                op0=ALU.is_ge, op1=ALU.add))
            link(nc.vector.scalar_tensor_tensor(out=row_f, in0=tmp_f, scalar=FAR, in1=row_i,
                                                op0=ALU.mult, op1=ALU.add))
            first, span = sched_f[:, :, 1], sched_f[:, :, 0]
            link(nc.vector.tensor_reduce(first, row_f, AX_X, ALU.min))
            link(nc.vector.tensor_scalar(first, first, float(N), None, ALU.min))
            for h in range(2):
                nc.vector.tensor_scalar(row_f[:, h, :], row_f[:, h, :], sched_f[:, h, 1:2], None,
                                        ALU.subtract).then_inc(s_rel, 1)
            dve.wait_ge(s_rel, 2)
            link(nc.vector.scalar_tensor_tensor(out=tmp_f, in0=tmp_f, scalar=-2 * FAR, in1=row_f,
                                                op0=ALU.mult, op1=ALU.add))
            link(nc.vector.tensor_reduce(span, tmp_f, AX_X, ALU.max))
            link(nc.vector.tensor_scalar(sched_i[:, :], span, 0.0, None, ALU.max))
            link(nc.vector.tensor_scalar(sched_i[:, :], sched_i[:, :], P.bit_length() - 1, None,
                                         ALU.arith_shift_right))
            nc.vector.tensor_scalar(span, sched_i[:, :], 1.0, None, ALU.add).then_inc(s_rel, 1)

            dve.wait_ge(s_sched, 1)
            dve.wait_ge(s_const, 4)
            shift = (4 * P).bit_length() - 1
            link(nc.vector.tensor_scalar(bound, bound, shift, shift, ALU.arith_shift_right,
                                         ALU.logical_shift_left))
            first_rows = sched.rearrange("o (g k) -> o g k", k=2)[:, LATE:NG, 1:2].rearrange("o g k -> o (g k)")
            link(nc.vector.tensor_tensor(in_order, first_rows, bound[:, 0:NG - LATE], ALU.is_ge))
            nc.vector.tensor_reduce(sorted_i, in_order, AX_X, ALU.min).then_inc(s_sorted, 1)
            dve.wait_ge(s_sorted, 1)
            ordered = dve.alloc_register("dve_ordered")
            dve.reg_load(ordered, sorted_i)
            dve.wait_ge(s_zero, 1)
            rounds = dve.alloc_register("dve_rounds")
            steps = dve.alloc_register("dve_steps")
            window = dve.alloc_register("dve_window")
            n_rounds = dve.alloc_register("dve_n_rounds")
            one = dve.alloc_register("dve_one")
            dve.reg_mov(one, 1)
            dve.reg_mov(rounds, 0)
            dve.reg_mov(steps, 0)

            def place(slot, tiles):
                for j in range(tiles):
                    last = nc.vector.tensor_scalar(onehot[:, j, :], iota[:, :], edge_slot[:, slot, j:j + 1],
                                                   edge_slot[:, slot, TG + j:TG + j + 1],
                                                   ALU.is_equal, ALU.mult)
                last.then_inc(s_onehot, 1)

            def add_window():
                dve.reg_add(rounds, rounds, 1)
                at = dve.snap(window, min_val=0, max_val=N)
                dve.wait_ge(s_window, rounds)
                return nc.vector.tensor_tensor(sumT[:, bass.ds(at, P)], sumT[:, bass.ds(at, P)],
                                               bank[0][:, 0:P], ALU.add)

            def layer_group(layer, beside=None):
                def add_group(g, i, slot, tiles):
                    dve.wait_ge(s_edge, g + (layer * NG + 1))
                    place(slot, tiles)
                    dve.reg_load(n_rounds, sched[0:1, bass.ds(g * 2, 1)])
                    dve.reg_load(window, sched[0:1, bass.ds(g * 2 + 1, 1)])
                    if beside is not None:
                        beside(g)
                    add_window()
                    with dve.If_lt(one, n_rounds):
                        with dve.Fori(1, n_rounds):
                            dve.reg_add(steps, steps, 1)
                            nc.vector.tensor_scalar(edge_slot[:, slot, 0:TG], edge_slot[:, slot, 0:TG],
                                                    float(P), None, ALU.subtract).then_inc(s_dec, 1)
                            dve.reg_add(window, window, P)
                            dve.reg_alu(window, window, N, ALU.min)
                            dve.wait_ge(s_dec, steps)
                            place(slot, tiles)
                            add_window()
                    nc.vector.memset(small[:, 7:8], 0.0).then_inc(s_group, 1)
                return add_group

            def item_indices(n, at, t_at):
                lane, neg = idx_l[:, 0, :], idx_l[:, 1, :]
                nc.vector.tensor_tensor(
                    pick, alias_i[:, bass.ds(at, IDX_L)].unsqueeze(2).broadcast_to([P, IDX_L, L]),
                    iota[:, 0:L].unsqueeze(1).broadcast_to([P, IDX_L, L]), ALU.is_equal).then_inc(s_pick, 1)
                dve.wait_ge(s_pick, n * 5 + 1)
                nc.vector.tensor_tensor(
                    pick, pick, items_i[:, bass.ds(t_at, L)].unsqueeze(1).broadcast_to([P, IDX_L, L]),
                    ALU.mult).then_inc(s_pick, 1)
                dve.wait_ge(s_pick, n * 5 + 2)
                nc.vector.tensor_reduce(lane, pick, AX_X, ALU.add).then_inc(s_pick, 1)
                dve.wait_ge(s_pick, n * 5 + 3)
                nc.vector.tensor_scalar(neg, lane, 0.0, float(N), ALU.is_lt, ALU.mult).then_inc(s_pick, 1)
                dve.wait_ge(s_pick, n * 5 + 4)
                nc.vector.tensor_tensor(lane, lane, neg, ALU.add).then_inc(s_pick, 1)
                dve.wait_ge(s_pick, n * 5 + 5)
                nc.vector.tensor_scalar(item_idx[:, bass.ds(at, IDX_L)], lane, 0.0, float(N - 1),
                                        ALU.max, ALU.min)

            def finish_steps(layer):
                def finish(q, part, base):
                    n = q + layer * NQ
                    w = quad(q) if isinstance(q, int) else 4
                    columns = sumT[:, bass.ds(q * (4 * P), w * P)]
                    if part == 0:
                        dve.wait_ge(s_group, base + 2)
                        nc.vector.tensor_scalar(quadT[:, 0:w * P], columns, 1.0, None, ALU.mult).then_inc(s_quadT, 1)
                        if layer == 0:
                            dve.wait_ge(s_quadT, n + 1)
                            nc.vector.tensor_scalar(columns.rearrange("p (j r) -> p j r", j=w),
                                                    iota[:, :].unsqueeze(1).broadcast_to([P, w, P]), 0.0, None,
                                                    ALU.mult).then_inc(s_zero, 1)
                        return
                    if part == 1:
                        dve.wait_ge(s_norm, n + 1)
                        nc.vector.tensor_scalar(h_norm[:, 0:w], h_norm[:, 0:w], EPS, None, ALU.max).then_inc(s_inv, 1)
                        h1_quad = seq0[:, bass.ds(q * (4 * D), w * D)]
                        base_quad = seq1[:, bass.ds(q * (4 * D), w * D)]
                        if layer == 1:
                            nc.vector.tensor_tensor(base_quad, base_quad, h1_quad, ALU.add)
                        dve.wait_ge(s_inv, n * 2 + 1)
                        nc.vector.reciprocal(h_inv[:, 0:w], h_norm[:, 0:w]).then_inc(s_inv, 1)
                        dve.wait_ge(s_inv, n * 2 + 2)
                        if layer == 0:
                            last = nc.vector.tensor_tensor(h1_quad.rearrange("p (j d) -> p j d", j=w),
                                                           bank[1][:, 0:w * D].rearrange("p (j d) -> p j d", j=w),
                                                           h_inv[:, 0:w].unsqueeze(2).broadcast_to([P, w, D]), ALU.mult)
                        else:
                            for j in range(w):
                                x = seq1[:, bass.ds(q * (4 * D) + j * D, D)]
                                last = nc.vector.scalar_tensor_tensor(
                                    out=x, in0=bank[1][:, j * D:(j + 1) * D], scalar=h_inv[:, j:j + 1], in1=x,
                                    op0=ALU.mult, op1=ALU.add)
                        last.then_inc(s_rows, 1)
                    elif part == 2:
                        dve.wait_ge(s_gnorm, q + 1)
                        nc.vector.tensor_scalar(g_norm[:, 0:w], g_norm[:, 0:w], (LAYERS + 1) * EPS, None,
                                                ALU.max).then_inc(s_ginv, 1)
                        dve.wait_ge(s_ginv, q * 3 + 1)
                        nc.vector.reciprocal(g_inv[:, 0:w], g_norm[:, 0:w]).then_inc(s_ginv, 1)
                        nc.vector.tensor_scalar(g_scale[:, 0:w], g_norm[:, 0:w], 1.0 / (LAYERS + 1), None,
                                                ALU.mult).then_inc(s_ginv, 1)
                        dve.wait_ge(s_ginv, q * 3 + 3)
                        nc.vector.tensor_tensor(gn_rows[:, 0:w, :],
                                                seq1[:, bass.ds(q * (4 * D), w * D)].rearrange("p (j d) -> p j d", j=w),
                                                g_inv[:, 0:w].unsqueeze(2).broadcast_to([P, w, D]),
                                                ALU.mult).then_inc(s_gn, 1)
                    else:
                        dve.wait_ge(s_gtc, q + 1)
                        nc.vector.tensor_scalar(columns, gn_T[:, 0:w * P], 1.0, None, ALU.mult).then_inc(s_gcol, 1)
                        dve.wait_ge(s_g1, q + 1)
                        dve.wait_ge(s_gst, q * 16 + 16)
                        nc.vector.tensor_tensor(g1_out[:, 0:w, :],
                                                bank[3][:, 0:w * D].rearrange("p (j d) -> p j d", j=w),
                                                g_scale[:, 0:w].unsqueeze(2).broadcast_to([P, w, D]),
                                                ALU.mult).then_inc(s_g1c, 1)
                return finish

            def last_group(layer):
                def rows_beside(g):
                    with dve.If_eq(ordered, one):
                        finish_steps(layer)(Q0, 1, None)
                return layer_group(layer, rows_beside)

            def masks():
                dve.wait_ge(s_sess_in, 48)
                link(nc.vector.tensor_scalar(mask[:, :], inputs_i, 0.0, None, ALU.not_equal))
                link(nc.vector.tensor_reduce(rcnt3[:, :], mask[:, :].rearrange("p (t l) -> p t l", t=T), AX_X,
                                             ALU.add))
                link(nc.vector.tensor_scalar(rcnt3[:, :], rcnt3[:, :], 3.0, None, ALU.mult))
                nc.vector.reciprocal(rcnt3[:, :], rcnt3[:, :]).then_inc(s_mask, 1)

            def with_indices(c, u):
                def body(k):
                    n, t = (c * IDX_U + u) * MG + k, u * MG + k
                    return layer_group(0, lambda g: item_indices(n, t * L + c * IDX_L, t * L))
                return [body(k) for k in range(MG)]

            layer_steps(dve, 0, layer_group(0), ordered, one, finish_steps(0), (1, 3),
                        {1: [(Q0, 0)], 3: [(Q1, 0), (Q1, 1)]}, with_indices, masks, last_group(0))
            dve.wait_ge(s_zero, NQ + 1)
            dve.wait_ge(s_base, 16 * (NQ - 1 + NT - 4 * (NQ - 1)))
            layer_steps(dve, 1, layer_group(1), ordered, one, finish_steps(1), (1, 3, 4, 7),
                        {1: [(Q0, 0)], 3: [(Q1, 0), (Q0, 2), (Q1, 1), (Q0, 3), (Q1, 2), (Q1, 3)]},
                        last_body=last_group(1))

            def step(s, par, half):
                own = seq[par]

                def weigh(c):
                    back, tp, ch = lagged(par, c, 2)
                    m = s * NC + (c - 2 - NC)
                    n = len(CH[ch])
                    l0 = CH[ch][0]
                    dve.wait_ge(s_beta, m + 1)
                    nc.vector.tensor_tensor(bm[:, ch % 2, 0:n], bank[4][:, tp * 64 + l0:tp * 64 + l0 + n],
                                            mask[:, bass.ds(s * L + (l0 - back * L), n)],
                                            ALU.mult).then_inc(s_bm, 1)
                    if not (isinstance(m, int) and m == 0):
                        dve.wait_ge(s_free, m)
                    dve.wait_ge(s_bm, m + 1)
                    for i, l in enumerate(CH[ch]):
                        acc, w = sess_acc[:, i, :], bm[:, ch % 2, i:i + 1]
                        if ch == 0:
                            last = nc.vector.tensor_scalar(acc, seq[tp][:, l, 0:D], w, None, ALU.mult)
                        else:
                            last = nc.vector.scalar_tensor_tensor(out=acc, in0=seq[tp][:, l, 0:D], scalar=w,
                                                                  in1=acc, op0=ALU.mult, op1=ALU.add)
                    last.then_inc(s_free, 1)

                for c in range(NC):
                    back, tp, ch = lagged(par, c, 1)
                    if have(s, back):
                        n = len(CH[ch])
                        m = s * NC + (c - 1 - NC)
                        slot = (par + c) % 2
                        dve.wait_ge(s_mm2, m + 1)
                        if ch == 0:
                            dve.wait_ge(s_qT, s)
                        if not (isinstance(m, int) and m < 2):
                            dve.wait_ge(s_beta, m - 1)
                        nc.vector.tensor_tensor(
                            two[:, slot, 0:n * P].rearrange("p (i b) -> p i b", i=n),
                            bank[2 + slot][:, 0:n * P].rearrange("p (i b) -> p i b", i=n),
                            qT[:, :].unsqueeze(1).broadcast_to([P, n, P]), ALU.add).then_inc(s_qadd, 1)
                    if c == 3 and have(s, 2):
                        dve.wait_ge(s_nn, s - 1)
                        nc.vector.tensor_scalar(small[:, 2:3], small[:, 1:2], (LAYERS + 1) * EPS, None,
                                                ALU.max).then_inc(s_sred, 1)
                        dve.wait_ge(s_sred, s * 2 - 3)
                        nc.vector.reciprocal(small[:, 3:4], small[:, 2:3]).then_inc(s_sred, 1)
                        dve.wait_ge(s_sred, s * 2 - 2)
                        nc.vector.tensor_scalar(small[:, 4 + par:5 + par], small[:, 3:4], W_K, None,
                                                ALU.mult).then_inc(s_scale, 1)
                    if have(s, 0):
                        full = 16 * len(CH[c])
                        dve.wait_ge(s_land[par][c], half * full + full)
                        if not (isinstance(s, int) and s == 0 and c == 0):
                            dve.wait_ge(s_hsum, s * NC + c)
                        for i, l in enumerate(CH[c]):
                            acc, mk = hs_acc[:, i, :], mask[:, bass.ds(s * L + l, 1)]
                            if c == 0:
                                last = nc.vector.tensor_scalar(acc, own[:, l, 0:D], mk, None, ALU.mult)
                            else:
                                last = nc.vector.scalar_tensor_tensor(out=acc, in0=own[:, l, 0:D], scalar=mk,
                                                                      in1=acc, op0=ALU.mult, op1=ALU.add)
                        last.then_inc(s_hsum, 1)
                    if c == NC - 1 and have(s, 0):
                        dve.wait_ge(s_hsum, s * NC + NC)
                        if have(s, 1):
                            dve.wait_ge(s_q, s)
                        nc.vector.tensor_reduce(hs_row[:, :], hs_acc[:, :, :].rearrange("p a d -> p d a"), AX_X,
                                                ALU.add).then_inc(s_hred, 1)
                        dve.wait_ge(s_hred, s + 1)
                        nc.vector.tensor_scalar(hs_row[:, :], hs_row[:, :], rcnt3[:, bass.ds(s, 1)], None,
                                                ALU.mult).then_inc(s_hs, 1)
                    if have(s, lagged(par, c, 2)[0]):
                        weigh(c)
                    if c == 1 and have(s, 2):
                        row = sessT[:, par, :]
                        dve.wait_ge(s_free, s * NC - NC)
                        nc.vector.tensor_reduce(row, sess_acc[:, :, :].rearrange("p a d -> p d a"), AX_X,
                                                ALU.add).then_inc(s_sess, 1)
                        dve.wait_ge(s_sess, s - 1)
                        nc.vector.tensor_tensor_reduce(out=square_dump[:, :], in0=row, in1=row,
                                                       scale=1.0, scalar=0.0, op0=ALU.mult, op1=ALU.add,
                                                       accum_out=small[:, 0:1]).then_inc(s_n2, 1)

            dve.wait_ge(s_mask, 1)
            session_steps(step, dve)

        @block.tensor
        def _(pe):
            pe.wait_ge(s_const, 3)
            n = 0
            for q, x, s, v in ((0, col_f, s_colf, 1), (1, row_f, s_rel, 2), (2, val_f, s_val, 48)):
                pe.wait_ge(s, v)
                for h in range(2):
                    for jj in range(2):
                        if n >= 4:
                            pe.wait_ge(s_tab, n - 3)
                        for j in range(4):
                            at = (4 * jj + j) * P
                            last = nc.tensor.transpose(bank[n % 4][:, j * HG:(j + 1) * HG],
                                                       x[:, h, at:at + P], ident[0:HG, 0:HG])
                        last.then_inc(s_tab_t, 1)
                        n += 1
            pe.wait_ge(s_rel, 3)
            for h in range(2):
                for k in range(2):
                    last = nc.tensor.transpose(bank[4][0:1, (2 * h + k) * HG:(2 * h + k + 1) * HG],
                                               sched_f[:, h, k:k + 1], ident[0:HG, 0:HG])
            last.then_inc(s_sched_t, 1)
            pe.wait_ge(s_w, 16 * 7)
            nc.tensor.transpose(bank[5][:, 0:L], pos_sb[0:L, :], ident[0:L, 0:L])
            nc.tensor.transpose(bank[6][:, 0:D], glu1_sb, ident[:, :])
            nc.tensor.transpose(bank[6][:, D:2 * D], glu2_sb, ident[:, :]).then_inc(s_w_t, 1)
            pe.wait_ge(s_w_c, 3)
            nc.tensor.matmul(bank[7][:, 0:L], w1a, hsT[:, 0:L], start=True, stop=True).then_inc(s_w_t, 1)

            pe.wait_ge(s_sched, 1)
            pe.wait_ge(s_tab, 12)
            pe.wait_ge(s_sorted, 1)
            ordered = pe.alloc_register("pe_ordered")
            pe.reg_load(ordered, sorted_i)
            rounds = pe.alloc_register("pe_rounds")
            n_rounds = pe.alloc_register("pe_n_rounds")
            one = pe.alloc_register("pe_one")
            pe.reg_mov(one, 1)
            pe.reg_mov(rounds, 0)
            for layer in range(LAYERS):
                def sum_group(g, i, slot, tiles):
                    pe.reg_load(n_rounds, sched[0:1, bass.ds(g * 2, 1)])
                    pe.reg_add(rounds, rounds, 1)
                    pe.wait_ge(s_onehot, rounds)
                    for j in range(tiles):
                        pe.wait_ge(s_gath[slot][j], landed(layer, i, slot, j))
                        last = nc.tensor.matmul(bank[0][:, 0:P], gath[:, slot, j, :], onehot[:, j, :],
                                                start=(j == 0), stop=(j == tiles - 1))
                    last.then_inc(s_window, 1)
                    with pe.If_lt(one, n_rounds):
                        with pe.Fori(1, n_rounds):
                            pe.reg_add(rounds, rounds, 1)
                            pe.wait_ge(s_onehot, rounds)
                            for j in range(tiles):
                                last = nc.tensor.matmul(bank[0][:, 0:P], gath[:, slot, j, :], onehot[:, j, :],
                                                        start=(j == 0), stop=(j == tiles - 1))
                            last.then_inc(s_window, 1)

                def finish(q, part, base):
                    w = quad(q) if isinstance(q, int) else 4
                    if part == 0:
                        pe.wait_ge(s_quadT, q + (layer * NQ + 1))
                        for j in range(w):
                            last = nc.tensor.transpose(bank[1][:, j * P:(j + 1) * P], quadT[:, j * P:(j + 1) * P],
                                                       ident[:, :])
                        last.then_inc(s_rowT, 1)
                    elif part == 1:
                        pe.wait_ge(s_gn, q + 1)
                        for j in range(w):
                            last = nc.tensor.transpose(bank[2][:, j * P:(j + 1) * P], gn_rows[:, j, :], ident[:, :])
                        last.then_inc(s_gt, 1)
                    else:
                        pe.wait_ge(s_gtc, q + 1)
                        for j in range(w):
                            last = nc.tensor.matmul(bank[3][:, j * D:(j + 1) * D], gn_T[:, j * P:(j + 1) * P],
                                                    w1b, start=True, stop=True)
                        last.then_inc(s_g1, 1)

                layer_steps(pe, layer, sum_group, ordered, one, finish, (2,) if layer == 0 else (2, 5, 6),
                            {2: [(Q0, 0)], 3: [(Q1, 0)] if layer == 0 else
                                [(Q1, 0), (Q0, 1), (Q0, 2), (Q1, 1), (Q1, 2)]})

            def step(s, par, half):
                def score(c, which):
                    back, tp, uh, ks = score_slot(par, half, c)
                    if not have(s, back) or which >= len(ks):
                        return
                    k = ks[which]
                    if k == 0:
                        pe.wait_ge(s_sessT, s - 1)
                    if not (isinstance(s, int) and s - back == 0 and k < 2):
                        pe.wait_ge(s_scored, s * NS + (max(k - 1, 0) - back * NS))
                    nc.tensor.matmul(bank[5 + k % 2][:, 0:SC], sessT[:, tp, :], sumT[:, k * SC:(k + 1) * SC],
                                     start=True, stop=True).then_inc(s_score, 1)

                if isinstance(s, int) and s == 2:
                    pe.wait_ge(s_gcol, NQ)
                for c in range(NC):
                    if c == 1 and have(s, 1):
                        pe.wait_ge(s_hsT, s)
                        nc.tensor.matmul(bank[7][:, P:2 * P], glu2T[:, :], hsT[:, :], start=True,
                                         stop=True).then_inc(s_q, 1)
                    if have(s, 1):
                        slot = (par + 1 + c) % 2
                        w = len(CH[c]) * P
                        m = s * NC + (c - NC)
                        pe.wait_ge(s_tanh, m + 1)
                        if not (isinstance(m, int) and m < 2):
                            pe.wait_ge(s_qadd, m - 1)
                        nc.tensor.matmul(bank[2 + slot][:, 0:w], glu1T[:, :], nh[:, c, 0:w],
                                         start=True, stop=True).then_inc(s_mm2, 1)
                    score(c, 0)
                    score(c, 1)
                    if c == 0 and have(s, 1):
                        pe.wait_ge(s_hs, s)
                        nc.tensor.transpose(bank[7][:, 0:P], hs_row[:, :], ident[:, :]).then_inc(s_hst, 1)
                    if c == 2 and have(s, 2):
                        pe.wait_ge(s_sess, s - 1)
                        if have(s, 1):
                            pe.wait_ge(s_qT, s)
                        nc.tensor.transpose(bank[7][:, 2 * P:3 * P], sessT[:, par, :], ident[:, :]).then_inc(s_sesst, 1)
                    back, tp, ch = lagged(par, c, 2)
                    if have(s, back):
                        m = s * NC + (c - 2 - NC)
                        slot = (par + 1 + c) % 2
                        pe.wait_ge(s_sig, m + 1)
                        if not (isinstance(m, int) and m == 0):
                            pe.wait_ge(s_bm, m)
                        for i, l in enumerate(CH[ch]):
                            last = nc.tensor.matmul(bank[4][:, tp * 64 + l:tp * 64 + l + 1],
                                                    two[:, slot, i * P:(i + 1) * P], w2c[:, :],
                                                    start=True, stop=True)
                        last.then_inc(s_beta, 1)
                    if have(s, 0):
                        full = 16 * len(CH[c])
                        pe.wait_ge(s_land[par][c], half * full + full)
                        if not (isinstance(s, int) and s == 0 and c < 2):
                            pe.wait_ge(s_tanh, s * NC + (c - 1))
                        for i, l in enumerate(CH[c]):
                            last = nc.tensor.transpose(bank[(par + c) % 2][:, i * P:(i + 1) * P],
                                                       seq[par][:, l, D:2 * D], ident[:, :])
                        last.then_inc(s_g1t, 1)

            session_steps(step, pe)


_INS = ['r_items', 'r_inputs', 'r_alias_inputs', 'L0_rec_adj_row', 'L0_rec_adj_col', 'L0_rec_adj_val', 'L0_rec_E',
        'L0_rec_pos_emb', 'L0_rec_w1', 'L0_rec_w2', 'L0_rec_glu1_w', 'L0_rec_glu1_b', 'L0_rec_glu2_w']


def kernel(**inputs):
    import numpy as _np
    import concourse.bacc as _bacc
    from concourse import mybir as _mybir
    from concourse.bass_utils import run_bass_kernel_spmd as _run

    nc = _bacc.Bacc("TRN2", target_bir_lowering=False, num_devices=1)
    arrays, args = {}, []
    for name in _INS:
        a = _np.ascontiguousarray(inputs[name])
        arrays[f"in_{name}_dram"] = a
        args.append(nc.dram_tensor(f"in_{name}_dram", a.shape, _mybir.dt.from_np(a.dtype), kind="ExternalInput").ap())
    shape = (inputs['r_items'].shape[0], inputs['L0_rec_E'].shape[0])
    args.append(nc.dram_tensor("out_0_dram", shape, _mybir.dt.float32, kind="ExternalOutput").ap())
    build(nc, *args)
    r = _run(nc, [arrays], core_ids=[0])
    return r.results[0]["out_0_dram"]
```
